# Optimizing a Trainium2 kernel written in Bass

```python
import numpy as np
import jax
import jax.numpy as jnp

def _softmax(x, axis=-1):
    return jax.nn.softmax(x, axis=axis)

def _gelu(x):
    return jax.nn.gelu(x, approximate=True)

def _silu(x):
    return jax.nn.silu(x)

def _sigmoid(x):
    return jax.nn.sigmoid(x)

def _layernorm(x, axis=-1, eps=1e-05):
    m = jnp.mean(x, axis=axis, keepdims=True)
    v = jnp.var(x, axis=axis, keepdims=True)
    return (x - m) / jnp.sqrt(v + eps)

def _scatter_add(tgt, idx, src, axis=0):
    return tgt.at[idx].add(src)

def _segment_sum(src, seg, n):
    return jax.ops.segment_sum(src, seg, n)
kernel_name = 'mk_adj_preln_d4_adj_r2_c607ce'

def setup_inputs(seed: int=0):
    np.random.seed(seed)
    _w = jnp.asarray

    def _rec_inputs():
        import jax
        import jax.numpy as jnp
        _gk = jax.random.key(seed)
        x = -0.0005207 + 1.001 * jax.random.normal(jax.random.fold_in(_gk, 1), (8192, 128), jnp.float32)
        _w = (1.0 + jnp.arange(8192, dtype=jnp.float32)) ** (-0.5)
        _w = _w / _w.mean()
        _pij = jnp.clip(0.00195312 * _w[:, None] * _w[None, :], 0.0, 1.0)
        _a = jax.random.uniform(jax.random.fold_in(_gk, 2), (8192, 8192)) < _pij
        adj = _a.astype(jnp.int32)
        return (x, adj)
    x, adj = _rec_inputs()

    def _L0_gnn_setup():
        import jax, jax.numpy as jnp
        import numpy as np
        N, D = (8192, 128)
        key = jax.random.key(seed)
        k1, k2 = jax.random.split(key)
        x = jax.random.normal(k1, (N, D), dtype=jnp.float32)
        adj = jax.random.randint(k2, (N, N), 0, 2, dtype=jnp.int32)
        return {'x': x, 'adj': adj}
    _L0_gnn_all = _L0_gnn_setup()
    _L0_gnn_in = {k: v for k, v in _L0_gnn_all.items() if k in ()}
    del _L0_gnn_all

    def _L1_gnn_setup():
        import jax, jax.numpy as jnp
        import numpy as np
        N = 6144
        IN_DIM = 128
        OUT_DIM = 128
        LR_SLOPE = 0.01
        NEG_INF = -9e+16
        key = jax.random.key(seed)
        k1, k2, k3, k4 = jax.random.split(key, 4)
        emb_mat = jax.random.normal(k1, (N, IN_DIM), dtype=jnp.float32)
        adj_mat = jax.random.randint(k2, (N, N), 0, 2, dtype=jnp.int32)
        W = jax.random.normal(k3, (OUT_DIM, IN_DIM), dtype=jnp.float32) * (2.0 / (IN_DIM + OUT_DIM)) ** 0.5
        a = jax.random.normal(k4, (2 * OUT_DIM, 1), dtype=jnp.float32) * (2.0 / (2 * OUT_DIM + 1)) ** 0.5
        return {'emb_mat': emb_mat, 'adj_mat': adj_mat, 'W': W, 'a': a}
    _L1_gnn_all = _L1_gnn_setup()
    _L1_gnn_in = {k: v for k, v in _L1_gnn_all.items() if k in ('W', 'a')}
    del _L1_gnn_all

    def _L2_gnn_setup():
        import jax, jax.numpy as jnp
        import numpy as np
        ALPHA = 0.2
        NEG_INF = -9000000000000000.0
        key = jax.random.key(seed)
        k1, k2, k3, k4 = jax.random.split(key, 4)
        N, F_IN, F_OUT = (4096, 128, 128)
        h = jax.random.normal(k1, (N, F_IN), dtype=jnp.float32)
        adj = jax.random.randint(k2, (N, N), 0, 2, dtype=jnp.int32)
        W = jax.random.normal(k3, (F_IN, F_OUT), dtype=jnp.float32) * (1.414 / np.sqrt(F_IN))
        a = jax.random.normal(k4, (2 * F_OUT, 1), dtype=jnp.float32) * (1.414 / np.sqrt(2 * F_OUT))
        return {'h': h, 'adj': adj, 'W': W, 'a': a}
    _L2_gnn_all = _L2_gnn_setup()
    _L2_gnn_in = {k: v for k, v in _L2_gnn_all.items() if k in ('W', 'a')}
    del _L2_gnn_all

    def _L3_gnn_setup():
        import jax, jax.numpy as jnp
        import numpy as np
        N = 4096
        IN = 128
        OUT = 128
        THR = 0.0001
        ALPHA = 0.2
        NEG = -1000000000.0
        key = jax.random.key(seed)
        k1, k2, k3, k4 = jax.random.split(key, 4)
        inp = jax.random.normal(k1, (N, IN), jnp.float32)
        W = jax.random.normal(k2, (IN, OUT), jnp.float32) * (1.414 * np.sqrt(2.0 / (IN + OUT)))
        a = jax.random.normal(k3, (2 * OUT, 1), jnp.float32) * (1.414 * np.sqrt(2.0 / (2 * OUT + 1)))
        adj = jax.random.randint(k4, (N, N), 0, 2, jnp.int32)
        return {'input': inp, 'W': W, 'a': a, 'adj': adj, 'M': N}
    _L3_gnn_all = _L3_gnn_setup()
    _L3_gnn_in = {k: v for k, v in _L3_gnn_all.items() if k in ('W', 'a')}
    del _L3_gnn_all
    return {'x': x, 'adj': adj, 'L1_gnn_W': _L1_gnn_in['W'], 'L1_gnn_a': _L1_gnn_in['a'], 'L2_gnn_W': _L2_gnn_in['W'], 'L2_gnn_a': _L2_gnn_in['a'], 'L3_gnn_W': _L3_gnn_in['W'], 'L3_gnn_a': _L3_gnn_in['a']}

def reference(x, adj, L1_gnn_W, L1_gnn_a, L2_gnn_W, L2_gnn_a, L3_gnn_W, L3_gnn_a):
    import jax
    import jax.numpy as jnp

    def _L0_gnn_ref(x, adj):
        import jax, jax.numpy as jnp
        import numpy as np
        N, D = (8192, 128)
        a = adj.astype(x.dtype)
        return x + jnp.matmul(a, x)

    def _L1_gnn_ref(emb_mat, adj_mat, W, a):
        import jax, jax.numpy as jnp
        import numpy as np
        N = 6144
        IN_DIM = 128
        OUT_DIM = 128
        LR_SLOPE = 0.01
        NEG_INF = -9e+16
        out_dim = W.shape[0]
        e_new = emb_mat @ W.T
        a1 = a[:out_dim, :]
        a2 = a[out_dim:, :]
        source_scores = e_new @ a1
        target_scores = e_new @ a2
        e = source_scores + target_scores.T
        e = jax.nn.leaky_relu(e, negative_slope=LR_SLOPE)
        e = jnp.where(adj_mat > 0, e, NEG_INF)
        attention = jax.nn.softmax(e, axis=-1)
        e_transf = attention @ e_new
        return jax.nn.relu(e_transf)

    def _L2_gnn_ref(h, adj, W, a):
        import jax, jax.numpy as jnp
        import numpy as np
        ALPHA = 0.2
        NEG_INF = -9000000000000000.0
        Wh = h @ W
        F_out = W.shape[1]
        e_src = Wh @ a[:F_out, 0]
        e_dst = Wh @ a[F_out:, 0]
        e = jax.nn.leaky_relu(e_src[:, None] + e_dst[None, :], negative_slope=ALPHA)
        attention = jax.nn.softmax(jnp.where(adj > 0, e, NEG_INF), axis=1)
        h_prime = attention @ Wh
        return h_prime

    def _L3_gnn_ref(input, W, a, adj, M):
        import jax, jax.numpy as jnp
        import numpy as np
        N = 4096
        IN = 128
        OUT = 128
        THR = 0.0001
        ALPHA = 0.2
        NEG = -1000000000.0
        h = input @ W
        a_src = a[:OUT, 0]
        a_dst = a[OUT:, 0]
        e = jax.nn.leaky_relu((h[:M] @ a_src)[:, None] + (h @ a_dst)[None, :], negative_slope=ALPHA)
        valid = (adj[:M] > 0) & (h.sum(axis=1) != 0)[None, :]
        att = jax.nn.softmax(jnp.where(valid, e, NEG), axis=1)
        att = jnp.where(valid, att, 0.0)
        L = valid.sum(axis=1).astype(h.dtype)
        top = att.max(axis=1)
        attention = jnp.where(att >= THR, att, 0.0) * L[:, None]
        attention = jnp.where((top > THR)[:, None], attention, 0.0)
        h_prime = attention @ h
        return jax.nn.elu(h[:M] + h_prime)
    h = jnp.maximum(_layernorm(x, axis=-1), 0.0)
    x = x + _L0_gnn_ref(h, adj)
    h = jnp.maximum(_layernorm(x, axis=-1), 0.0)
    x = x + _L1_gnn_ref(h, adj, L1_gnn_W, L1_gnn_a)
    h = jnp.maximum(_layernorm(x, axis=-1), 0.0)
    x = x + _L2_gnn_ref(h, adj, L2_gnn_W, L2_gnn_a)
    h = jnp.maximum(_layernorm(x, axis=-1), 0.0)
    x = x + _L3_gnn_ref(h, L3_gnn_W, L3_gnn_a, adj, 8192)
    return x

_drawn_inputs = setup_inputs


def setup_inputs(seed=0):
    import zlib

    import numpy as np

    out = dict(_drawn_inputs(seed))
    spreads = {}
    factors = {'L1_gnn_a': 6.962}
    for name, (base, spread) in spreads.items():
        noise = np.random.default_rng([zlib.crc32(name.encode()), seed]).standard_normal(out[name].shape)
        drawn = base * np.exp(spread * noise) if base else spread * noise
        out[name] = jnp.asarray(drawn.astype(out[name].dtype))
    for name, factor in factors.items():
        out[name] = (out[name] * factor).astype(out[name].dtype)
    return out
```

```python
from contextlib import ExitStack, nullcontext

import concourse.bass as bass
from concourse import mybir
import numpy as np

ALU = mybir.AluOpType
ACT = mybir.ActivationFunctionType
AX_X = mybir.AxisListType.X
F32 = mybir.dt.float32
F16 = mybir.dt.float16
BF16 = mybir.dt.bfloat16
F8 = mybir.dt.float8e4
I32 = mybir.dt.int32
U8 = mybir.dt.uint8
U16 = mybir.dt.uint16

P = 128
D = 128
NORM = D
E = D + 1
EP = E + 1
MASK = 64
MASK_F8 = 2.0
THR = 1e-4
SLOPE = {1: 0.01, 2: 0.2, 3: 0.2}
WINDOW = {1: 70.0, 2: 40.0, 3: 40.0}
ROW_SEEN = {l: float(np.exp(-w - 0.5)) for l, w in WINDOW.items()}
MAX_LEVELS = 1 << 12
H_SCALE = 1024.0
NORM_SCALE = 16384.0
E_BOUND = 512.0
EPS = 1e-5
ROW_SUM_LEAST = 2.0 ** -60
LEAST = 1e-30
ADJ_COLS = 2048
UB = 4
EXP_BITS, MANT_BITS, ONE_BITS = 0x7F800000, 0x007FFFFF, 0x3F800000
RING = 8
B16_RING = 4


def build_layers(nc, x_in, adj_in, w1, a1, w2, a2, w3, a3, x_out):
    N = x_in.shape[0]
    NB = N // P
    GB = 8
    G = NB // GB
    GW = GB * P
    CJ = 4
    BODY = 8
    NBODY = NB // BODY
    TILES = G * NB
    NCOL = N // ADJ_COLS
    CB = ADJ_COLS // P
    LAYERS = (1, 2, 3)

    mask_dram = nc.dram_tensor("mask_dram", [NB, P, NB, P], U8, kind="Internal").ap()
    row_dram = [nc.dram_tensor(f"row_dram{l}", [3, NB, P], F32, kind="Internal").ap() for l in range(4)]

    with ExitStack() as ctx:
        def sb(name, shape, dt):
            return ctx.enter_context(nc.sbuf_tensor(name, shape, dt))

        def sem(name):
            return ctx.enter_context(nc.semaphore(name))

        def per_layer(name, layers=LAYERS):
            return {l: sem(f"{name}{l}") for l in layers}

        x = sb("x", [P, NB, D], F32)
        e = sb("e", [P, NB, EP], F32)
        xu = sb("xu", [P, NB, 2, EP], F16)
        xl = sb("xl", [P, NB, 2, EP], F16)
        xl_now = sb("xl_now", [P, 2, CJ, 2, EP], F16)
        ring = sb("ring", [P, 24 * 1024], U8)
        work = sb("work", [P, GB * 258], F32)
        comb = sb("comb", [P, GB, EP], F32)
        y = sb("y", [P, GB, D], F32)
        thr = sb("thr", [P, 2, GW], F32)
        masks = sb("masks", [P, 2, GB, CJ * P], U8)
        step8 = sb("step8", [P, 4, GW], U8)
        ident = sb("ident", [P, P], F32)
        identb = sb("identb", [P, P], BF16)
        ones = sb("ones", [P, P], F32)
        w_raw = sb("w_raw", [P, 3, D], F32)
        w_e = sb("w_e", [P, 3, D], F32)
        w_a = sb("w_a", [P, 3, 2], F32)
        a_col = sb("a_col", [P, 3, 2], F32)
        mean = sb("mean", [P, D], F32)
        vec = {n: sb(f"v_{n}", [P, NB], F32) for n in (
            "mu", "rstd", "tmp", "tmp2", "s", "t", "keep", "v", "vl", "pow2", "mant", "clow",
            "lnc", "empty", "done", "new", "f", "z", "rest", "valid")}
        one = {n: sb(f"c_{n}", [P, 3], F32) for n in ("n2", "p2", "scale", "unscale", "knorm")}
        tm = sb("tm", [P, 2], F32)
        tmr = sb("tmr", [P, 2], F32)
        top = sb("top", [P, 1], F32)
        levels_f = sb("levels_f", [P, 1], F32)
        levels = sb("levels", [P, 3], I32)
        rows = sb("rows", [NB, 2, P], F32)
        vz = sb("vz", [P, NB, 10], BF16)
        vz_now = sb("vz_now", [P, 2, CJ, 10], BF16)
        zr = sb("zr", [P, NB, 3], F32)
        psum = ctx.enter_context(nc.psum_tensor("psum", [P, 8, 512], F32))

        tmp = work[:, 0:2 * GB * E].rearrange("p (s b w) -> p s b w", s=2, b=GB)
        stage = work[:, :].rearrange("p (b w) -> p b w", b=GB)
        zs = work[:, 0:NB * 10].rearrange("p (b w) -> p b w", b=NB)
        stats = work[:, 0:NB * 6].rearrange("p (b w) -> p b w", b=NB)
        w_t = work[:, 1024:1024 + 3 * D].rearrange("p (k d) -> p k d", k=3)
        B8 = ring[:, 0:8192].rearrange("p (s w) -> p s w", s=RING)
        C8 = ring[:, 8192:16384].rearrange("p (s w) -> p s w", s=RING)
        B16 = ring[:, 16384:24576].bitcast(BF16).rearrange("p (s w) -> p s w", s=B16_RING)
        AT = ring[:, 0:2 * N].rearrange("p (s w) -> p s w", s=2)
        hT = ring[:, 0:4096].bitcast(F32).rearrange("p (s w) -> p s w", s=2)
        hs = ring[:, 16384:20480].bitcast(F32).rearrange("p (s w) -> p s w", s=2)
        hr = ring[:, 20480:24576].bitcast(F32).rearrange("p (s w) -> p s w", s=2)
        adj_sb = e[:, :, :].rearrange("p b w -> p (b w)")[:, 0:NCOL * ADJ_COLS].bitcast(I32).rearrange("p (c w) -> p c w", c=NCOL)
        adj_bf = xl[:, :, :, :].rearrange("p a b c -> p (a b c)")[:, 0:NCOL * ADJ_COLS].bitcast(BF16).rearrange("p (c w) -> p c w", c=NCOL)

        def words(ap):
            return ap.bitcast(U16).rearrange("p (b w) -> p b w", b=GB)

        def mask_words(slot, k):
            return masks[:, slot, :, k * P:(k + 1) * P].bitcast(U16)

        def bank16(bank):
            return psum[:, bank, :].bitcast(BF16)

        def over(v, width):
            return v.unsqueeze(2).to_broadcast([P, v.shape[1], width])

        x_loaded, w_loaded, const_ready = sem("x_loaded"), sem("w_loaded"), sem("const_ready")
        w_trans, w_copied, w_proj, norm2_ready, w_norm, w_ready = (sem(n) for n in (
            "w_trans", "w_copied", "w_proj", "norm2_ready", "w_norm", "w_ready"))
        adj_loaded = [sem(f"adj_loaded{c}") for c in range(NCOL)]
        adj_masked, transposed = sem("adj_masked"), sem("transposed")
        evacuated = sem("evacuated")
        sums_done = sem("sums_done")
        sums_read = sem("sums_read")
        mask_stored = [sem(f"mask_stored{s}") for s in range(2)]
        h_used = sem("h_used")
        ALL = (0,) + LAYERS
        var_ready, std_ready, h_raw, h_ready, hi_ready = (per_layer(n, ALL) for n in (
            "var_ready", "std_ready", "h_raw", "h_ready", "hi_ready"))
        h_trans, hT_ready, e_made, e_ready = (per_layer(n) for n in ("h_trans", "hT_ready", "e_made", "e_ready"))
        t_range, t_range_all, levels_ready = (per_layer(n) for n in ("t_range", "t_range_all", "levels_ready"))
        neg_s, neg_s_trans, neg_s_row, neg_s_stored = (per_layer(n) for n in ("neg_s", "neg_s_trans", "neg_s_row", "neg_s_stored"))
        gaps_ready, exps_ready, scales_ready = (per_layer(n) for n in ("gaps_ready", "exps_ready", "scales_ready"))
        prod_ready, hi_done, parts_ready = (per_layer(n) for n in ("prod_ready", "hi_done", "parts_ready"))
        pe_gated, sp_gated = sem("pe_gated"), sem("sp_gated")
        thr_ready = per_layer("thr_ready")
        masks_ready = {l: [sem(f"masks_ready{l}_{s}") for s in range(2)] for l in LAYERS}
        stepped, kept8, upper8 = per_layer("stepped"), sem("kept8"), per_layer("upper8")
        lower8 = per_layer("lower8")
        upper16 = per_layer("upper16")
        xl_loaded = {l: [sem(f"xl_loaded{l}_{s}") for s in range(2)] for l in LAYERS}
        tile_done = per_layer("tile_done")
        bank_done = per_layer("bank_done")
        bank_read = per_layer("bank_read")
        stage_used = per_layer("stage_used")
        mean_added = per_layer("mean_added", (1, 2))
        z_parts, z_thr_ready, z_stepped, z_upper8, z_read = (sem(n) for n in (
            "z_parts", "z_thr_ready", "z_stepped", "z_upper8", "z_read"))
        z_columns = sem("z_columns")
        z_tile = sem("z_tile")
        z_masks_ready = [sem(f"z_masks_ready{s}") for s in range(2)]
        row_sum, row_ln, cuts, cuts_trans, cut_rows, cut_stored = (sem(n) for n in (
            "row_sum", "row_ln", "cuts", "cuts_trans", "cut_rows", "cut_stored"))
        elu_neg, elu_exp = sem("elu_neg"), sem("elu_exp")
        x_final, x_stored = sem("x_final"), sem("x_stored")

        def n_levels(eng, l):
            eng.wait_ge(levels_ready[l], 1)
            return eng.value_load(levels[0:1, l - 1:l], min_val=1, max_val=MAX_LEVELS)

        block = ctx.enter_context(nc.Block())

        @block.sync
        def _(sp):
            def gate():
                sp.nop().then_inc(sp_gated, 1)

            sp.dma_start(x[:, :, :], x_in.rearrange("(b p) d -> p b d", p=P)).then_inc(x_loaded, 16)
            for k, (w, a) in enumerate(((w1, a1), (w2, a2), (w3, a3))):
                sp.dma_start(w_raw[:, k, :], w).then_inc(w_loaded, 16)
                with nc.allow_non_contiguous_dma(reason="256 numbers"):
                    sp.dma_start(a_col[:, k, :], a.rearrange("(h p) o -> p (h o)", p=P)).then_inc(w_loaded, 16)

            adj_rows = adj_in.rearrange("(b p) (c w) -> c b p w", p=P, w=ADJ_COLS)
            for first in (True, False):
                with nullcontext(0) if first else sp.Fori(1, NB) as b:
                    for c in range(NCOL):
                        if not first:
                            sp.wait_ge(adj_masked, (b - 1) * NCOL + c + 1)
                        sp.dma_start(adj_sb[:, c, :], adj_rows[c, bass.ds(b, 1)].rearrange("a p w -> (a p) w")) \
                            .then_inc(adj_loaded[c], 16)

            def load_masks(ready, slot, g, k):
                sp.dma_start(masks[:, slot, :, :], mask_dram[bass.ds(g * GB, GB), :, bass.ds(k * CJ, CJ), :].rearrange(
                    "b p j i -> p b (j i)")).then_inc(ready[slot], 16)

            def load_thr(l, which, row, g, ready):
                sp.dma_start(thr[:, which, :], row_dram[l][row, bass.ds(g * GB, GB), :].rearrange("b p -> (b p)")
                             .partition_broadcast(P)).then_inc(ready, 16)

            for l in LAYERS:
                sp.wait_ge(neg_s_row[l], 1)
                sp.dma_start(row_dram[l][0, :, :], rows[:, 0, :]).then_inc(neg_s_stored[l], 16)
                sp.wait_ge(neg_s_stored[l], 16)
                if l == 1:
                    for s in range(2):
                        sp.wait_ge(mask_stored[s], 16 * (NB // 2) + 16)
                n_lev = n_levels(sp, l)
                with sp.Fori(0, n_lev) as lev:
                    if l == 3:
                        sp.wait_ge(lower8[3], lev * TILES + 2 * CJ)
                        gate()
                        with sp.Fori(0, G) as g:
                            for first in (True, False):
                                with nullcontext(0) if first else sp.Fori(1, NBODY) as c:
                                    for k in range(2):
                                        sp.wait_ge(z_tile, lev * TILES + g * NB + c * BODY + (k + 1) * CJ)
                                        gate()
                                        load_masks(z_masks_ready, k, g, c * 2 + k)
                                        if first and k == 0:
                                            sp.wait_ge(z_stepped, lev * TILES + g * NB + 1)
                                            gate()
                                            load_thr(3, 0, 0, g, z_thr_ready)
                        sp.wait_ge(cut_rows, lev + 1)
                        gate()
                        sp.dma_start(row_dram[3][1:3, :, :].rearrange("r b p -> b r p"), rows[:, :, :]) \
                            .then_inc(cut_stored, 16)
                        sp.wait_ge(cut_stored, lev * 16 + 32)
                        gate()
                    with sp.Fori(0, G) as g:
                        for first in (True, False):
                            with nullcontext(0) if first else sp.Fori(1, NBODY) as c:
                                for k in range(2):
                                    sp.wait_ge(lower8[l], lev * TILES + g * NB + c * BODY + (k + 1) * CJ)
                                    gate()
                                    load_masks(masks_ready[l], k, g, c * 2 + k)
                                    if first and k == 0:
                                        sp.wait_ge(stepped[l], lev * TILES + g * NB + 1)
                                        gate()
                                        if l == 3:
                                            load_thr(3, 0, 1, g, thr_ready[3])
                                            load_thr(3, 1, 2, g, thr_ready[3])
                                        else:
                                            load_thr(l, 0, 0, g, thr_ready[l])
            sp.wait_ge(x_final, 1)
            sp.dma_start(x_out.rearrange("(b p) d -> p b d", p=P), x[:, :, :]).then_inc(x_stored, 16)
            sp.wait_ge(x_stored, 16)

        @block.gpsimd
        def _(pool):
            for s, n in ([(evacuated, 4), (sums_done, 2), (sums_read, 2), (z_tile, RING), (z_stepped, 1), (z_upper8, 1), (z_read, 1),
                          (mask_stored[0], 16), (mask_stored[1], 16), (cut_stored, 16)]
                         + [(s, n) for l in LAYERS for s, n in (
                             (lower8[l], 2 * CJ), (upper16[l], RING), (tile_done[l], RING), (bank_read[l], GB),
                             (stage_used[l], 1), (stepped[l], 1))]):
                pool.nop().then_inc(s, n)
            nc.gpsimd.memset(ones[:, :], 1.0)
            nc.gpsimd.memset(ident[:, :], 0.0)
            pool.drain()
            nc.gpsimd.affine_select(out=ident[:, :], in_=ident[:, :], compare_op=ALU.not_equal, fill=1.0, base=0,
                                    pattern=[[-1, P]], channel_multiplier=1)
            pool.drain()
            nc.gpsimd.tensor_copy(identb[:, :], ident[:, :])
            nc.gpsimd.memset(xu[:, :, 0, NORM:NORM + 1], 1.0)
            nc.gpsimd.memset(xu[:, :, 1, NORM:NORM + 1], 0.0)
            nc.gpsimd.memset(xl[:, :, :, E:EP], 0.0)
            pool.drain().then_inc(const_ready, 1)

            pool.wait_ge(adj_masked, NB * NCOL)
            nc.gpsimd.memset(e[:, :, NORM:NORM + 1], NORM_SCALE)
            pool.drain().then_inc(const_ready, 1)

            for l in (1, 2):
                one_pass = lambda b: e[:, b * GB:(b + 1) * GB, 0:D]
                pool.wait_ge(t_range[l], 1)
                nc.gpsimd.partition_all_reduce(tmr[:, :], tm[:, :], P, bass.bass_isa.ReduceOp.max) \
                    .then_inc(t_range_all[l], 1)
                pool.wait_ge(e_ready[l], NB // UB)
                nc.gpsimd.tensor_tensor(y[:, :, :], one_pass(0), one_pass(1), ALU.add)
                for b in range(2, NB // GB):
                    pool.drain()
                    nc.gpsimd.tensor_tensor(y[:, :, :], y[:, :, :], one_pass(b), ALU.add)
                half = GB // 2
                while half:
                    pool.drain()
                    nc.gpsimd.tensor_tensor(y[:, 0:half, :], y[:, 0:half, :], y[:, half:2 * half, :], ALU.add)
                    half //= 2
                pool.drain()
                nc.gpsimd.partition_all_reduce(mean[:, :], y[:, 0, :], P, bass.bass_isa.ReduceOp.add)
                pool.drain()
                nc.gpsimd.tensor_scalar(mean[:, :], mean[:, :], one["unscale"][:, l - 1:l], 1.0 / N, ALU.mult, ALU.mult)
                if l == 1:
                    pool.drain()
                    nc.gpsimd.tensor_scalar(mean[:, :], mean[:, :], 0.0, None, ALU.max)
                with pool.Fori(0, G) as g:
                    pool.drain()
                    nc.gpsimd.tensor_tensor(y[:, :, :], mean[:, :].unsqueeze(1).to_broadcast([P, GB, D]),
                                            over(vec["empty"][:, bass.ds(g * GB, GB)], D), ALU.mult)
                    pool.drain()
                    nc.gpsimd.tensor_tensor(x[:, bass.ds(g * GB, GB), :], x[:, bass.ds(g * GB, GB), :], y[:, :, :], ALU.add)
                pool.drain().then_inc(mean_added[l], 1)
            pool.wait_ge(t_range[3], 1)
            nc.gpsimd.partition_all_reduce(tmr[:, :], tm[:, :], P, bass.bass_isa.ReduceOp.max) \
                .then_inc(t_range_all[3], 1)

        @block.tensor
        def _(pe):
            def gate():
                pe.nop().then_inc(pe_gated, 1)

            pe.wait_ge(w_loaded, 16 * 6)
            pe.wait_ge(const_ready, 1)
            for k in range(3):
                mm = nc.tensor.transpose(psum[:, 5, k * P:(k + 1) * P], w_raw[:, k, :], ident[:, :])
            mm.then_inc(w_trans, 1)
            pe.wait_ge(w_copied, 1)
            for k in range(3):
                w_out_in = w_raw[:, k, :] if k == 0 else w_t[:, k, :]
                mm = nc.tensor.matmul(psum[:, 6, 2 * k:2 * k + 2], w_out_in, a_col[:, k, :], start=True, stop=True)
                mm = nc.tensor.matmul(psum[:, 7, k * P:(k + 1) * P], ones[:, :], w_e[:, k, :], start=True, stop=True)
            mm.then_inc(w_proj, 1)

            def transposes(b, c):
                for h in range(2):
                    if h == 0:
                        pe.wait_ge(adj_masked, b * NCOL + c + 1)
                    pe.wait_ge(evacuated, b * 2 * NCOL + 2 * c + h + 1)
                    for k in range(8):
                        at = (8 * h + k) * P
                        mm = nc.tensor.transpose(bank16(2 * (c % 2) + h)[:, k * P:(k + 1) * P],
                                                 adj_bf[:, c, at:at + P], identb[:, :])
                    mm.then_inc(transposed, 1)

            def sums(b, slot, c):
                if c == 0:
                    pe.wait_ge(sums_read, b + 1)
                pe.wait_ge(evacuated, b * 2 * NCOL + 2 * c + 2 + 4)
                gate()
                for k in range(16):
                    j = 16 * c + k
                    for part in range(2):
                        mm = nc.tensor.matmul(psum[:, 4 + slot, 0:E], AT[:, slot, j * P:(j + 1) * P].bitcast(F8),
                                              xu[:, j, part, 0:E], start=(j == 0 and part == 0),
                                              stop=(j == NB - 1 and part == 1), skip_group_check=True)
                if c == NCOL - 1:
                    mm.then_inc(sums_done, 1)

            pe.wait_ge(w_norm, 1)
            for c in range(NCOL):
                transposes(0, c)
            pe.wait_ge(h_used, NB // UB)
            with pe.Fori(0, NB // 2 - 1) as i:
                for u in range(2):
                    for c in range(NCOL):
                        transposes(2 * i + 1 + u, c)
                        sums(2 * i + u, u, c)
            for c in range(NCOL):
                transposes(NB - 1, c)
                sums(NB - 2, 0, c)
            for c in range(NCOL):
                sums(NB - 1, 1, c)

            for l in LAYERS:
                k_w = l - 1
                if l == 1:
                    pe.wait_ge(w_ready, 1)

                def transpose_h(unit, s, first):
                    pe.wait_ge(h_ready[l], unit + 1)
                    if not first:
                        pe.wait_ge(hT_ready[l], unit - 1)
                    for k in range(UB):
                        mm = nc.tensor.transpose(psum[:, s, k * P:(k + 1) * P], hr[:, s, k * P:(k + 1) * P], ident[:, :])
                    mm.then_inc(h_trans[l], 1)

                def project(unit, s, first):
                    pe.wait_ge(hT_ready[l], unit + 1)
                    if not first:
                        pe.wait_ge(e_ready[l], unit - 1)
                    for k in range(UB):
                        lhsT = hT[:, s, k * P:(k + 1) * P]
                        nc.tensor.matmul(psum[:, 2 + s, k * P:(k + 1) * P], lhsT, w_e[:, k_w, :], start=True, stop=True)
                        mm = nc.tensor.matmul(psum[:, 4, bass.ds((unit * UB + k) * 2, 2)], lhsT, w_a[:, k_w, :],
                                              start=True, stop=True)
                    mm.then_inc(e_made[l], 1)

                NU = NB // UB
                for u in range(2):
                    transpose_h(u, u, True)
                for u in range(2):
                    project(u, u, True)
                    transpose_h(u + 2, u, False)
                with pe.Fori(1, NU // 2 - 1) as i:
                    for u in range(2):
                        project(2 * i + u, u, False)
                        transpose_h(2 * i + u + 2, u, False)
                for u in range(2):
                    project(NU - 2 + u, u, False)
                pe.wait_ge(neg_s[l], 1)
                nc.tensor.transpose(psum[0:NB, 5, 0:P], vec["tmp"][:, :], ident[:, :]).then_inc(neg_s_trans[l], 1)

                n_lev = n_levels(pe, l)
                with pe.Fori(0, n_lev) as lev:
                    if l == 3:
                        pe.wait_ge(z_parts, lev + 1)
                        gate()
                        with pe.Fori(0, G) as g:
                            pe.wait_ge(z_read, lev * G + g + 1)
                            for first in (True, False):
                                with nullcontext(0) if first else pe.Fori(1, NBODY) as c:
                                    for u in range(BODY):
                                        n = lev * TILES + g * NB + c * BODY + u
                                        pe.wait_ge(z_upper8, n + 2)
                                        if u % CJ == 0:
                                            pe.wait_ge(z_columns, lev * (TILES // CJ) + g * (NB // CJ) + c * 2 + u // CJ + 1)
                                        gate()
                                        for b in range(GB):
                                            i0 = u % CJ * P
                                            nc.tensor.matmul(psum[:, b, 0:6], B8[:, u, b * P:(b + 1) * P].bitcast(F8),
                                                             vz_now[:, u // CJ, u % CJ, 0:6],
                                                             start=(first and u == 0), stop=True, skip_group_check=True)
                                            mm = nc.tensor.matmul(psum[:, b, 6:10],
                                                                  masks[:, u // CJ, b, i0:i0 + P].bitcast(F8),
                                                                  vz_now[:, u // CJ, u % CJ, 6:10],
                                                                  start=False, stop=True, skip_group_check=True)
                                        mm.then_inc(z_tile, 1)
                        pe.wait_ge(cuts, lev + 1)
                        gate()
                        nc.tensor.transpose(psum[0:NB, 0, 0:P], vec["tmp"][:, :], ident[:, :])
                        nc.tensor.transpose(psum[0:NB, 0, P:2 * P], vec["tmp2"][:, :], ident[:, :]).then_inc(cuts_trans, 1)
                        pe.wait_ge(cut_rows, lev + 1)
                        gate()
                    with pe.Fori(0, G) as g:
                        for first in (True, False):
                            with nullcontext(0) if first else pe.Fori(1, NBODY) as c:
                                pe.wait_ge(parts_ready[l], lev * NBODY + c + 1)
                                for u in range(BODY):
                                    n = lev * TILES + g * NB + c * BODY + u
                                    pe.wait_ge(lower8[l], n + 1 + 2 * CJ)
                                    if u % CJ == 0:
                                        pe.wait_ge(xl_loaded[l][u // CJ], 16 * (lev * G * NBODY + g * NBODY + c + 1))
                                    pe.wait_ge(upper16[l], n + 1 + RING)
                                    for b in range(GB):
                                        if first and u == 0:
                                            pe.wait_ge(bank_read[l], lev * NB + g * GB + b + 1)
                                        for part in range(2):
                                            mm = nc.tensor.matmul(
                                                psum[:, b, 0:E], B16[:, u % B16_RING, b * P:(b + 1) * P],
                                                xu[:, bass.ds(c * BODY + u, 1), part, 0:E].rearrange("p a w -> p (a w)"),
                                                start=(first and u == 0 and part == 0), stop=True, skip_group_check=True)
                                        for part in range(2):
                                            mm = nc.tensor.matmul(
                                                psum[:, b, E:2 * E], C8[:, u, b * P:(b + 1) * P].bitcast(F8),
                                                xl_now[:, u // CJ, u % CJ, part, 0:E],
                                                start=False, stop=True, skip_group_check=True)
                                        if u == BODY - 1 and b < GB - 1:
                                            mm.then_inc(bank_done[l], 1)
                                    mm.then_inc(tile_done[l], 1)

        @block.scalar
        def _(act):
            act.wait_ge(norm2_ready, 1)
            nc.scalar.activation(one["n2"][:, :], one["n2"][:, :], ACT.Sqrt).then_inc(w_norm, 1)

            def normalise(l):
                act.wait_ge(var_ready[l], 1)
                nc.scalar.activation(vec["rstd"][:, :], vec["tmp2"][:, :], ACT.Sqrt).then_inc(std_ready[l], 1)

            def relu(l, unit, s, first):
                act.wait_ge(h_raw[l], unit + 1)
                if not first:
                    act.wait_ge(h_used if l == 0 else h_trans[l], unit - 1)
                nc.scalar.activation(hr[:, s, :], hs[:, s, :], ACT.Relu).then_inc(h_ready[l], 1)

            def blocks(s):
                return hr[:, s, :].rearrange("p (b d) -> p b d", b=UB)

            normalise(0)
            for first in (True, False):
                with nullcontext(0) if first else act.Fori(1, NB // UB // 2) as i:
                    for s in range(2):
                        unit = 2 * i + s
                        relu(0, unit, s, first)
                        act.wait_ge(h_ready[0], unit + 1)
                        nc.scalar.activation(xu[:, bass.ds(unit * UB, UB), 0, 0:D], blocks(s), ACT.Copy, scale=H_SCALE) \
                            .then_inc(hi_ready[0], 1)

            with act.Fori(0, NB // 2) as i:
                for s in range(2):
                    b = 2 * i + s
                    act.wait_ge(mask_stored[s], 16 * i + 16)
                    act.wait_ge(sums_done, b + 1)
                    for c in range(NCOL):
                        for h in range(2):
                            act.wait_ge(transposed, b * 2 * NCOL + 2 * c + h + 1)
                            at = (2 * c + h) * 8 * P
                            nc.scalar.activation(AT[:, s, at:at + 8 * P], bank16(2 * (c % 2) + h), ACT.Copy,
                                                 scale=float(MASK)).then_inc(evacuated, 1)
                    act.wait_ge(evacuated, (b + 1) * 2 * NCOL + 4)
                    act.dma_start(mask_dram[bass.ds(b, 1)].rearrange("a p j i -> p (a j i)"), AT[:, s, :]) \
                        .then_inc(mask_stored[s], 16)

            for l in LAYERS:
                slope = SLOPE[l]
                normalise(l)

                def e_out(unit, s):
                    act.wait_ge(e_made[l], unit + 1)
                    nc.scalar.activation(e[:, bass.ds(unit * UB, UB), 0:D],
                                         psum[:, 2 + s, :].rearrange("p (b d) -> p b d", b=UB), ACT.Copy) \
                        .then_inc(e_ready[l], 1)

                NU = NB // UB
                for u in range(2):
                    relu(l, u, u, True)
                with act.Fori(0, NU // 2 - 1) as i:
                    for u in range(2):
                        relu(l, 2 * i + u + 2, u, False)
                        e_out(2 * i + u, u)
                for u in range(2):
                    e_out(NU - 2 + u, u)

                n_lev = n_levels(act, l)
                with act.Fori(0, n_lev) as lev:
                    act.wait_ge(gaps_ready[l], lev + 1)
                    nc.scalar.activation(vec["v"][:, :], vec["tmp2"][:, :], ACT.Exp)
                    nc.scalar.activation(vec["vl"][:, :], vec["tmp2"][:, :], ACT.Exp, scale=slope)
                    nc.scalar.activation(vec["clow"][:, :], vec["lnc"][:, :], ACT.Exp).then_inc(exps_ready[l], 1)

                    if l == 3:
                        def z_chunk_columns(g, c):
                            for k in range(2):
                                act.wait_ge(z_tile, lev * TILES + g * NB + c * BODY + (k + 1) * CJ)
                                nc.scalar.activation(vz_now[:, k, :, :], vz[:, bass.ds(c * BODY + k * CJ, CJ), :],
                                                     ACT.Copy).then_inc(z_columns, 1)

                        act.wait_ge(z_parts, lev + 1)
                        with act.Fori(0, G) as g:
                            with act.Fori(0, NBODY) as c:
                                z_chunk_columns(g, c)
                            act.wait_ge(z_tile, lev * TILES + (g + 1) * NB + RING)
                            nc.scalar.activation(zs[:, bass.ds(g * GB, GB), :], psum[:, :, 0:10], ACT.Copy).then_inc(z_read, 1)
                        act.wait_ge(row_sum, lev + 1)
                        nc.scalar.activation(vec["z"][:, :], vec["z"][:, :], ACT.Ln).then_inc(row_ln, 1)

                    def hi(c):
                        for k, half in enumerate((xu, xl)):
                            act.wait_ge(prod_ready[l], lev * 2 * NBODY + 2 * c + k + 1)
                            nc.scalar.activation(half[:, bass.ds(c * GB, GB), 0, 0:E], tmp[:, k, :, :], ACT.Copy) \
                                .then_inc(hi_done[l], 1)

                    def scale_upper(g, c, tiles):
                        for u in tiles:
                            n = lev * TILES + g * NB + c * BODY + u
                            if u % CJ == 0:
                                act.wait_ge(tile_done[l], n - CJ + RING)
                                act.dma_start(xl_now[:, u // CJ], xl[:, bass.ds(c * BODY + u, CJ)]) \
                                    .then_inc(xl_loaded[l][u // CJ], 16)
                            act.wait_ge(upper8[l], n + 1)
                            act.wait_ge(tile_done[l], n + 1 + RING - B16_RING)
                            nc.scalar.activation(B16[:, u % B16_RING, :], B8[:, u, :], ACT.Copy,
                                                 scale=vec["pow2"][:, bass.ds(c * BODY + u, 1)]).then_inc(upper16[l], 1)

                    def read_banks(g):
                        act.wait_ge(stage_used[l], lev * G + g + 1)
                        for b in range(GB):
                            if b < GB - 1:
                                act.wait_ge(bank_done[l], (GB - 1) * (lev * G * NBODY + (g + 1) * NBODY - 1) + b + 1)
                            else:
                                act.wait_ge(tile_done[l], lev * TILES + (g + 1) * NB + RING)
                            nc.scalar.activation(stage[:, b, :], psum[:, b, 0:2 * E], ACT.Copy).then_inc(bank_read[l], 1)

                    def elu(g):
                        act.wait_ge(elu_neg, lev * G + g + 1)
                        nc.scalar.activation(comb[:, :, 0:D], comb[:, :, 0:D], ACT.Exp).then_inc(elu_exp, 1)

                    act.wait_ge(scales_ready[l], lev + 1)
                    for first in (True, False):
                        with nullcontext(0) if first else act.Fori(1, NBODY) as c:
                            hi(c)
                            act.wait_ge(parts_ready[l], lev * NBODY + c + 1)
                            scale_upper(0, c, range(BODY))
                    with act.Fori(1, G) as g:
                        scale_upper(g, 0, range(B16_RING - 1))
                        read_banks(g - 1)
                        scale_upper(g, 0, range(B16_RING - 1, BODY))
                        if l == 3:
                            elu(g - 1)
                        with act.Fori(1, NBODY) as c:
                            scale_upper(g, c, range(BODY))
                    read_banks(G - 1)
                    if l == 3:
                        elu(G - 1)

        @block.vector
        def _(dve):
            ve = nc.vector
            dve.wait_ge(w_loaded, 16 * 6)
            dve.wait_ge(w_trans, 1)
            ve.tensor_copy(w_t[:, :, :], psum[:, 5, 0:3 * P].rearrange("p (k d) -> p k d", k=3))
            dve.drain()
            in_out = [w_t[:, 0, :], w_raw[:, 1, :], w_raw[:, 2, :]]
            for k in range(3):
                ve.tensor_tensor(w_e[:, k, :], in_out[k], in_out[k], ALU.mult)
            dve.drain().then_inc(w_copied, 1)
            dve.wait_ge(w_proj, 1)
            ve.tensor_copy(w_a[:, :, :], psum[:, 6, 0:6].rearrange("p (k d) -> p k d", k=3))
            ve.tensor_reduce(one["n2"][:, :], psum[:, 7, 0:3 * P].rearrange("p (k d) -> p k d", k=3), AX_X, ALU.max)
            dve.drain().then_inc(norm2_ready, 1)
            dve.wait_ge(w_norm, 1)
            ve.tensor_scalar(one["n2"][:, :], one["n2"][:, :], LEAST, None, ALU.max)
            dve.drain()
            ve.tensor_scalar(one["p2"][:, :].bitcast(I32), one["n2"][:, :].bitcast(I32), EXP_BITS, None, ALU.bitwise_and)
            dve.drain()
            ve.tensor_scalar(one["unscale"][:, :], one["p2"][:, :], 1.0 / E_BOUND, None, ALU.mult)
            dve.drain()
            ve.reciprocal(one["scale"][:, :], one["unscale"][:, :])
            ve.tensor_scalar(one["knorm"][:, :], one["unscale"][:, :], NORM_SCALE, None, ALU.mult)
            dve.drain()
            for k in range(3):
                ve.tensor_scalar(w_e[:, k, :], in_out[k], one["scale"][:, k:k + 1], None, ALU.mult)
            dve.drain().then_inc(w_ready, 1)

            def statistics(l):
                with dve.Fori(0, NB // 8) as i:
                    for k in range(8):
                        ve.bn_stats(stats[:, bass.ds(i * 8 + k, 1), :].rearrange("p a w -> p (a w)"),
                                    x[:, bass.ds(i * 8 + k, 1), :].rearrange("p a w -> p (a w)"))
                dve.drain()
                m0, q0, m1, q1 = (stats[:, :, k] for k in (1, 2, 4, 5))
                ve.tensor_tensor(vec["mu"][:, :], m0, m1, ALU.add)
                ve.tensor_tensor(vec["tmp"][:, :], m0, m1, ALU.subtract)
                ve.tensor_tensor(vec["tmp2"][:, :], q0, q1, ALU.add)
                dve.drain()
                ve.tensor_scalar(vec["mu"][:, :], vec["mu"][:, :], 0.5, None, ALU.mult)
                ve.tensor_tensor(vec["tmp"][:, :], vec["tmp"][:, :], vec["tmp"][:, :], ALU.mult)
                dve.drain()
                ve.scalar_tensor_tensor(out=vec["tmp2"][:, :], in0=vec["tmp"][:, :], scalar=D / 4.0,
                                        in1=vec["tmp2"][:, :], op0=ALU.mult, op1=ALU.add)
                dve.drain()
                ve.tensor_scalar(vec["tmp2"][:, :], vec["tmp2"][:, :], 1.0 / D, EPS, ALU.mult, ALU.add)
                dve.drain().then_inc(var_ready[l], 1)
                dve.wait_ge(std_ready[l], 1)
                ve.reciprocal(vec["rstd"][:, :], vec["rstd"][:, :])
                dve.drain()

            def centre(l, unit, s, first):
                if not first:
                    dve.wait_ge(h_ready[l], unit - 1)
                for k in range(UB):
                    b = unit * UB + k
                    out = ve.tensor_scalar(hs[:, s, k * P:(k + 1) * P], x[:, bass.ds(b, 1), :].rearrange("p a w -> p (a w)"),
                                           vec["mu"][:, bass.ds(b, 1)], vec["rstd"][:, bass.ds(b, 1)],
                                           ALU.subtract, ALU.mult)
                out.then_inc(h_raw[l], 1)

            dve.wait_ge(x_loaded, 16)
            statistics(0)
            for first in (True, False):
                with nullcontext(0) if first else dve.Fori(1, NB // UB // 2) as i:
                    for s in range(2):
                        centre(0, 2 * i + s, s, first)
                    for s in range(2):
                        unit = 2 * i + s
                        dve.wait_ge(hi_ready[0], unit + 1)
                        hb = hr[:, s, :].rearrange("p (b d) -> p b d", b=UB)
                        at = bass.ds(unit * UB, UB)
                        ve.scalar_tensor_tensor(out=xu[:, at, 1, 0:D], in0=hb, scalar=H_SCALE, in1=xu[:, at, 0, 0:D],
                                                op0=ALU.mult, op1=ALU.subtract)
                        ve.tensor_tensor(x[:, at, :], x[:, at, :], hb, ALU.add).then_inc(h_used, 1)

            def make_mask(b, c, first=False):
                dve.wait_ge(adj_loaded[c], 16 * b + 16)
                if not first:
                    dve.wait_ge(transposed, (b - 1) * 2 * NCOL + 2 * c + 2)
                ve.tensor_scalar(adj_bf[:, c, :], adj_sb[:, c, :], 0.0, None, ALU.is_gt).then_inc(adj_masked, 1)

            def add_sums(b, slot):
                dve.wait_ge(sums_done, b + 1 + 2)
                at = bass.ds(b, 1)
                xb = x[:, at, :].rearrange("p a w -> p (a w)")
                ve.scalar_tensor_tensor(out=xb, in0=psum[:, 4 + slot, 0:D], scalar=1.0 / (H_SCALE * MASK_F8),
                                        in1=xb, op0=ALU.mult, op1=ALU.add)
                ve.tensor_scalar(vec["empty"][:, at], psum[:, 4 + slot, NORM:NORM + 1], 0.0, None,
                                 ALU.is_equal).then_inc(sums_read, 1)

            dve.wait_ge(const_ready, 1)
            for b in range(2):
                for c in range(NCOL):
                    make_mask(b, c, first=(b == 0))
            with dve.Fori(1, NB // 2) as i:
                for s in range(2):
                    for c in range(NCOL):
                        make_mask(2 * i + s, c)
                        if c == 1:
                            add_sums(2 * i + s - 2, s)
            for s in range(2):
                add_sums(NB - 2 + s, s)
            dve.drain()

            def first_pass(lev):
                v3 = [(vec["v"], vz[:, :, 0:3]), (vec["vl"], vz[:, :, 3:6])]
                for value, parts in v3:
                    ve.tensor_copy(parts[:, :, 0], value[:, :])
                    dve.drain()
                    ve.tensor_tensor(vec["rest"][:, :], value[:, :], parts[:, :, 0], ALU.subtract)
                    dve.drain()
                    ve.tensor_copy(parts[:, :, 1], vec["rest"][:, :])
                    dve.drain()
                    ve.tensor_tensor(vec["rest"][:, :], vec["rest"][:, :], parts[:, :, 1], ALU.subtract)
                    dve.drain()
                    ve.tensor_copy(parts[:, :, 2], vec["rest"][:, :])
                    dve.drain()
                ve.tensor_copy(vz[:, :, 6:9], vz[:, :, 3:6])
                ve.tensor_copy(vz[:, :, 9], vec["valid"][:, :])
                dve.drain().then_inc(z_parts, 1)

                def cut_upper(g, c, new_group):
                    if new_group:
                        dve.wait_ge(z_thr_ready, 16 * (lev * G + g + 1))
                    for u0 in range(0, BODY, 2):
                        if u0 % CJ == 0:
                            dve.wait_ge(z_masks_ready[u0 // CJ], 16 * (lev * G * NBODY + g * NBODY + c + 1))
                        pair = [(u, lev * TILES + g * NB + c * BODY + u) for u in (u0, u0 + 1)]
                        dve.wait_ge(z_upper8, pair[0][1] + (1 if u0 == 0 else -1))
                        for u, n in pair:
                            ve.tensor_scalar(step8[:, u % 4, :], thr[:, 0, :], vec["t"][:, bass.ds(c * BODY + u, 1)],
                                             float(MASK), ALU.is_le, ALU.mult).then_inc(z_stepped, 1)
                        for u, n in pair:
                            dve.wait_ge(z_stepped, n + 2)
                            dve.wait_ge(z_tile, n + 1)
                            ve.tensor_tensor(words(B8[:, u, :]), words(step8[:, u % 4, :]), mask_words(u // CJ, u % CJ),
                                             ALU.bitwise_and).then_inc(z_upper8, 1)

                with dve.Fori(0, G) as g:
                    cut_upper(g, 0, True)
                    with dve.Fori(1, NBODY) as c:
                        cut_upper(g, c, False)

                dve.wait_ge(z_read, lev * G + G + 1)
                ve.tensor_reduce(zr[:, :, :], zs[:, :, 0:9].rearrange("p b (k w) -> p b k w", w=3), AX_X, ALU.add)
                dve.drain()
                ve.tensor_tensor(vec["rest"][:, :], zr[:, :, 2], zr[:, :, 1], ALU.subtract)
                dve.drain()
                ve.tensor_tensor(vec["rest"][:, :], vec["rest"][:, :], vec["clow"][:, :], ALU.mult)
                dve.drain()
                ve.scalar_tensor_tensor(out=vec["rest"][:, :], in0=zr[:, :, 0], scalar=1.0 / MASK_F8,
                                        in1=vec["rest"][:, :], op0=ALU.mult, op1=ALU.add)
                dve.drain()
                ve.tensor_scalar(vec["z"][:, :], vec["rest"][:, :], ROW_SUM_LEAST, None, ALU.max)
                ve.tensor_scalar(vec["new"][:, :], vec["rest"][:, :], ROW_SEEN[3], None, ALU.is_ge)
                ve.tensor_scalar(vec["tmp"][:, :], zs[:, :, 9], 0.0, None, ALU.is_equal)
                dve.drain()
                ve.reciprocal(vec["f"][:, :], vec["z"][:, :])
                ve.tensor_tensor(vec["new"][:, :], vec["new"][:, :], vec["tmp"][:, :], ALU.max)
                dve.drain().then_inc(row_sum, 1)
                ve.tensor_tensor(vec["new"][:, :], vec["new"][:, :], vec["done"][:, :], ALU.is_gt)
                ve.tensor_tensor(vec["f"][:, :], vec["f"][:, :], zs[:, :, 9], ALU.mult)
                dve.drain()
                ve.tensor_tensor(vec["done"][:, :], vec["done"][:, :], vec["new"][:, :], ALU.max)
                ve.tensor_scalar(vec["f"][:, :], vec["f"][:, :], one["unscale"][:, 2:3], 1.0 / MASK_F8, ALU.mult, ALU.mult)
                dve.drain()
                ve.tensor_tensor(vec["f"][:, :], vec["f"][:, :], vec["new"][:, :], ALU.mult)
                dve.wait_ge(row_ln, lev + 1)
                ve.tensor_scalar(vec["z"][:, :], vec["z"][:, :], float(np.log(THR)), None, ALU.add)
                dve.drain()
                ve.tensor_tensor(vec["rest"][:, :], vec["z"][:, :], vec["lnc"][:, :], ALU.subtract)
                ve.tensor_scalar(vec["tmp"][:, :], vec["z"][:, :], top[:, 0:1], None, ALU.add)
                dve.drain()
                ve.tensor_scalar(vec["rest"][:, :], vec["rest"][:, :], 1.0 / SLOPE[3], top[:, 0:1], ALU.mult, ALU.add)
                ve.scalar_tensor_tensor(out=vec["tmp"][:, :], in0=vec["s"][:, :], scalar=-1.0, in1=vec["tmp"][:, :],
                                        op0=ALU.mult, op1=ALU.max)
                dve.drain()
                ve.tensor_tensor(vec["tmp2"][:, :], vec["rest"][:, :], vec["tmp"][:, :], ALU.min)
                dve.drain().then_inc(cuts, 1)
                dve.wait_ge(cuts_trans, lev + 1)
                dve.wait_ge(cut_stored, 16 * lev + 16)
                ve.tensor_copy(rows[:, :, :], psum[0:NB, 0, 0:2 * P].rearrange("b (k p) -> b k p", k=2)).then_inc(cut_rows, 1)

            for l in LAYERS:
                slope, kw = SLOPE[l], l - 1
                statistics(l)
                if l == 1:
                    for s in range(2):
                        dve.wait_ge(mask_stored[s], 16 * (NB // 2) + 16)
                NU = NB // UB

                def copy_hT(unit, s, first):
                    dve.wait_ge(h_trans[l], unit + 1)
                    if not first:
                        dve.wait_ge(e_made[l], unit - 1)
                    ve.tensor_copy(hT[:, s, :], psum[:, s, :]).then_inc(hT_ready[l], 1)

                for u in range(2):
                    centre(l, u, u, True)
                for u in range(2):
                    centre(l, u + 2, u, False)
                    copy_hT(u, u, True)
                with dve.Fori(1, NU // 2 - 1) as i:
                    for u in range(2):
                        centre(l, 2 * i + u + 2, u, False)
                        copy_hT(2 * i + u, u, False)
                for u in range(2):
                    copy_hT(NU - 2 + u, u, False)

                dve.wait_ge(e_made[l], NU)
                st = psum[:, 4, 0:2 * NB].rearrange("p (b k) -> p b k", k=2)
                ve.tensor_copy(vec["s"][:, :], st[:, :, 0])
                ve.tensor_copy(vec["t"][:, :], st[:, :, 1])
                ve.tensor_scalar(vec["tmp"][:, :], st[:, :, 0], -1.0, None, ALU.mult)
                ve.tensor_scalar(vec["tmp2"][:, :], st[:, :, 1], -1.0, None, ALU.mult)
                dve.drain().then_inc(neg_s[l], 1)
                ve.tensor_reduce(tm[:, 0:1], vec["t"][:, :], AX_X, ALU.max)
                ve.tensor_reduce(tm[:, 1:2], vec["tmp2"][:, :], AX_X, ALU.max)
                dve.drain().then_inc(t_range[l], 1)
                ve.memset(vec["done"][:, :], 0.0)
                dve.wait_ge(neg_s_trans[l], 1)
                ve.tensor_copy(rows[:, 0, :], psum[0:NB, 5, 0:P]).then_inc(neg_s_row[l], 1)
                if l == 3:
                    dve.wait_ge(e_ready[l], NU)
                    ve.tensor_reduce(vec["valid"][:, :], e[:, :, 0:D], AX_X, ALU.add)
                    dve.drain()
                    ve.tensor_scalar(vec["valid"][:, :], vec["valid"][:, :], 0.0, None, ALU.not_equal)
                dve.wait_ge(t_range_all[l], 1)
                ve.tensor_copy(top[:, :], tmr[:, 0:1])
                ve.tensor_tensor(levels_f[:, :], tmr[:, 0:1], tmr[:, 1:2], ALU.add)
                dve.drain()
                ve.tensor_scalar(levels_f[:, :], levels_f[:, :], 1.0 / WINDOW[l], 1.0, ALU.mult, ALU.add)
                dve.drain()
                ve.tensor_scalar(levels_f[:, :], levels_f[:, :], float(MAX_LEVELS), None, ALU.min)
                dve.drain()
                ve.tensor_copy(levels[:, kw:kw + 1], levels_f[:, :])
                dve.drain().then_inc(levels_ready[l], 1)

                n_lev = n_levels(dve, l)
                with dve.Fori(0, n_lev) as lev:
                    ve.tensor_scalar(vec["tmp2"][:, :], vec["t"][:, :], top[:, 0:1], None, ALU.subtract)
                    ve.tensor_scalar(vec["lnc"][:, :], vec["s"][:, :], top[:, 0:1], 0.0, ALU.add, ALU.max)
                    dve.drain()
                    ve.tensor_scalar(vec["keep"][:, :], vec["tmp2"][:, :], 0.0, None, ALU.is_le)
                    dve.drain()
                    ve.tensor_scalar(vec["tmp2"][:, :], vec["tmp2"][:, :], 0.0, None, ALU.min)
                    ve.tensor_scalar(vec["lnc"][:, :], vec["lnc"][:, :], slope - 1.0, None, ALU.mult)
                    if l == 3:
                        ve.tensor_tensor(vec["keep"][:, :], vec["keep"][:, :], vec["valid"][:, :], ALU.mult)
                    dve.drain().then_inc(gaps_ready[l], 1)
                    dve.wait_ge(exps_ready[l], lev + 1)
                    ve.tensor_tensor(vec["v"][:, :], vec["v"][:, :], vec["keep"][:, :], ALU.mult)
                    ve.tensor_tensor(vec["vl"][:, :], vec["vl"][:, :], vec["keep"][:, :], ALU.mult)
                    ve.tensor_scalar(vec["clow"][:, :], vec["clow"][:, :], 1.0 / MASK_F8, None, ALU.mult)
                    dve.drain()
                    ve.tensor_scalar(vec["pow2"][:, :].bitcast(I32), vec["v"][:, :].bitcast(I32), EXP_BITS, None,
                                     ALU.bitwise_and)
                    ve.tensor_scalar(vec["mant"][:, :].bitcast(I32), vec["v"][:, :].bitcast(I32), MANT_BITS, ONE_BITS,
                                     ALU.bitwise_and, ALU.bitwise_or)
                    dve.drain()
                    ve.tensor_scalar(vec["pow2"][:, :], vec["pow2"][:, :], 1.0 / MASK, None, ALU.mult)
                    dve.drain().then_inc(scales_ready[l], 1)

                    if l == 3:
                        first_pass(lev)

                    def parts(c):
                        at = bass.ds(c * GB, GB)
                        for k, scale in enumerate((vec["mant"], vec["vl"])):
                            ve.tensor_tensor(tmp[:, k, :, :], e[:, at, 0:E], over(scale[:, at], E),
                                             ALU.mult).then_inc(prod_ready[l], 1)
                        for k, half in enumerate((xu, xl)):
                            dve.wait_ge(hi_done[l], lev * 2 * NBODY + 2 * c + k + 1)
                            out = ve.tensor_tensor(half[:, at, 1, 0:E], tmp[:, k, :, :], half[:, at, 0, 0:E], ALU.subtract)
                        out.then_inc(parts_ready[l], 1)

                    def cut_masks(g, c, new_group):
                        if new_group:
                            dve.wait_ge(thr_ready[l], 16 * (2 if l == 3 else 1) * (lev * G + g + 1))
                        for u0 in range(0, BODY, 2):
                            if u0 % CJ == 0:
                                dve.wait_ge(masks_ready[l][u0 // CJ], 16 * (lev * G * NBODY + g * NBODY + c + 1))
                            pair = [(u, lev * TILES + g * NB + c * BODY + u) for u in (u0, u0 + 1)]
                            t_of = lambda u: vec["t"][:, bass.ds(c * BODY + u, 1)]
                            for u, n in pair:
                                if l == 3:
                                    ve.tensor_scalar(step8[:, 2 + u % 2, :], thr[:, 1, :], t_of(u), float(MASK),
                                                     ALU.is_le, ALU.mult)
                                ve.tensor_scalar(step8[:, u % 2, :], thr[:, 0, :], t_of(u), float(MASK),
                                                 ALU.is_le, ALU.mult).then_inc(stepped[l], 1)
                            if l == 3:
                                for u, n in pair:
                                    dve.wait_ge(stepped[l], n + 2)
                                    dve.wait_ge(tile_done[l], n + 1)
                                    ve.tensor_tensor(words(C8[:, u, :]), words(step8[:, 2 + u % 2, :]),
                                                     mask_words(u // CJ, u % CJ), ALU.bitwise_and).then_inc(kept8, 1)
                            for u, n in pair:
                                dve.wait_ge(kept8 if l == 3 else stepped[l], n + (1 if l == 3 else 2))
                                dve.wait_ge(upper16[l], n + 1)
                                ve.tensor_tensor(words(B8[:, u, :]), words(step8[:, u % 2, :]),
                                                 words(C8[:, u, :]) if l == 3 else mask_words(u // CJ, u % CJ),
                                                 ALU.bitwise_and).then_inc(upper8[l], 1)
                            for u, n in pair:
                                dve.wait_ge(upper8[l], n + 1)
                                if l != 3:
                                    dve.wait_ge(tile_done[l], n + 1)
                                ve.tensor_tensor(words(C8[:, u, :]), words(B8[:, u, :]),
                                                 words(C8[:, u, :]) if l == 3 else mask_words(u // CJ, u % CJ),
                                                 ALU.bitwise_xor).then_inc(lower8[l], 1)

                    def finish(g):
                        at = bass.ds(g * GB, GB)
                        dve.wait_ge(bank_read[l], lev * NB + (g + 1) * GB + GB)
                        if l != 3:
                            dve.wait_ge(mean_added[l], 1)
                        ve.tensor_tensor(comb[:, :, 0:E], stage[:, :, E:2 * E], over(vec["clow"][:, at], E), ALU.mult)
                        dve.drain()
                        ve.tensor_tensor(comb[:, :, 0:E], comb[:, :, 0:E], stage[:, :, 0:E], ALU.add)
                        dve.drain().then_inc(stage_used[l], 1)
                        if l != 3:
                            new, f, done = vec["new"][:, at], vec["f"][:, at], vec["done"][:, at]
                            z = comb[:, :, NORM]
                            ve.tensor_scalar(new, z, ROW_SEEN[l] * NORM_SCALE, None, ALU.is_ge)
                            ve.tensor_scalar(f, z, LEAST, None, ALU.max)
                            dve.drain()
                            ve.tensor_tensor(new, new, done, ALU.is_gt)
                            ve.reciprocal(f, f)
                            dve.drain()
                            ve.tensor_tensor(done, done, new, ALU.max)
                            ve.scalar_tensor_tensor(out=f, in0=f, scalar=one["knorm"][:, kw:kw + 1], in1=new,
                                                    op0=ALU.mult, op1=ALU.mult)
                            dve.drain()
                        ve.tensor_tensor(y[:, :, :], comb[:, :, 0:D], over(vec["f"][:, at], D), ALU.mult)
                        dve.drain()
                        if l == 1:
                            ve.tensor_scalar(y[:, :, :], y[:, :, :], 0.0, None, ALU.max)
                            dve.drain()
                        if l == 3:
                            flat = y[:, :, :].rearrange("p b d -> p (b d)")
                            ve.scalar_tensor_tensor(out=y[:, :, :], in0=e[:, at, 0:D], scalar=one["unscale"][:, kw:kw + 1],
                                                    in1=y[:, :, :], op0=ALU.mult, op1=ALU.add)
                            dve.drain()
                            ve.tensor_scalar(comb[:, :, 0:D], y[:, :, :], 0.0, None, ALU.min).then_inc(elu_neg, 1)
                            dve.wait_ge(elu_exp, lev * G + g + 1)
                            ve.scalar_tensor_tensor(out=y[:, :, :], in0=y[:, :, :], scalar=0.0, in1=comb[:, :, 0:D],
                                                    op0=ALU.max, op1=ALU.add)
                            dve.drain()
                            ve.scalar_tensor_tensor(out=y[:, :, :], in0=y[:, :, :], scalar=-1.0,
                                                    in1=over(vec["new"][:, at], D), op0=ALU.add, op1=ALU.mult)
                            dve.drain()
                        ve.tensor_tensor(x[:, at, :], x[:, at, :], y[:, :, :], ALU.add)

                    if l == 1:
                        dve.wait_ge(const_ready, 2)
                    dve.wait_ge(e_ready[l], NU)
                    for first in (True, False):
                        with nullcontext(0) if first else dve.Fori(1, NBODY) as c:
                            parts(c)
                            cut_masks(0, c, first)
                    with dve.Fori(1, G) as g:
                        cut_masks(g, 0, True)
                        finish(g - 1)
                        with dve.Fori(1, NBODY) as c:
                            cut_masks(g, c, False)
                    finish(G - 1)
                    dve.drain()
                    ve.tensor_scalar(top[:, :], top[:, :], -WINDOW[l], None, ALU.add)
                    dve.drain()
            dve.drain().then_inc(x_final, 1)


_INS = ["x", "adj", "L1_gnn_W", "L1_gnn_a", "L2_gnn_W", "L2_gnn_a", "L3_gnn_W", "L3_gnn_a"]


def kernel(**inputs):
    import numpy as _np
    import concourse.bacc as _bacc
    from concourse import mybir as _mybir
    from concourse.bass_utils import run_bass_kernel_spmd as _run

    nc = _bacc.Bacc("TRN2", target_bir_lowering=False, num_devices=1)
    arrays, args = {}, []
    for name in _INS:
        a = _np.ascontiguousarray(inputs[name])
        arrays[f"in_{name}_dram"] = a
        args.append(nc.dram_tensor(f"in_{name}_dram", a.shape, _mybir.dt.from_np(a.dtype), kind="ExternalInput").ap())
    out = nc.dram_tensor("out_0_dram", inputs["x"].shape, _mybir.dt.from_np(_np.dtype("float32")), kind="ExternalOutput").ap()
    build_layers(nc, *args, out)
    r = _run(nc, [arrays], core_ids=[0])
    return r.results[0]["out_0_dram"]
```

```python
from contextlib import ExitStack, nullcontext

import concourse.bass as bass
from concourse import mybir
import numpy as np

ALU = mybir.AluOpType
ACT = mybir.ActivationFunctionType
AX_X = mybir.AxisListType.X
F32 = mybir.dt.float32
F16 = mybir.dt.float16
BF16 = mybir.dt.bfloat16
F8 = mybir.dt.float8e4
I32 = mybir.dt.int32
U8 = mybir.dt.uint8
U16 = mybir.dt.uint16

P = 128
D = 128
NORM = D
E = D + 1
EP = E + 1
MASK = 64
MASK_F8 = 2.0
THR = 1e-4
SLOPE = {1: 0.01, 2: 0.2, 3: 0.2}
WINDOW = {1: 70.0, 2: 40.0, 3: 40.0}
ROW_SEEN = {l: float(np.exp(-w - 0.5)) for l, w in WINDOW.items()}
MAX_LEVELS = 1 << 12
H_SCALE = 1024.0
NORM_SCALE = 16384.0
E_BOUND = 512.0
EPS = 1e-5
ROW_SUM_LEAST = 2.0 ** -60
FAR = 2.0 ** 60
LEAST = 1e-30
ADJ_COLS = 2048
UB = 4
EXP_BITS, MANT_BITS, ONE_BITS = 0x7F800000, 0x007FFFFF, 0x3F800000
RING = 8
B16_RING = 4


def build_layers(nc, x_in, adj_in, w1, a1, w2, a2, w3, a3, x_out):
    N = x_in.shape[0]
    NB = N // P
    GB = 8
    G = NB // GB
    GW = GB * P
    CJ = 4
    BODY = 8
    NBODY = NB // BODY
    TILES = G * NB
    NCOL = N // ADJ_COLS
    CB = ADJ_COLS // P
    LAYERS = (1, 2, 3)
    N_ACT = 7
    Z_ACT = 5
    Z_DVE = BODY - Z_ACT

    OCT = NB // 8
    HO = OCT // 2
    QG = GB // 2
    LEAD = 3
    PLANES = 8 // NCOL

    mask_dram = nc.dram_tensor("mask_dram", [NB // 2, P, OCT, 2 * P], U8, kind="Internal").ap()
    row_dram = [nc.dram_tensor(f"row_dram{l}", [3, NB, P], F32, kind="Internal").ap() for l in range(4)]

    with ExitStack() as ctx:
        def sb(name, shape, dt):
            return ctx.enter_context(nc.sbuf_tensor(name, shape, dt))

        def sem(name):
            return ctx.enter_context(nc.semaphore(name))

        def per_layer(name, layers=LAYERS):
            return {l: sem(f"{name}{l}") for l in layers}

        x = sb("x", [P, NB, D], F32)
        e = sb("e", [P, NB, EP], F32)
        xu = sb("xu", [P, NB, 2, EP], F16)
        xl = sb("xl", [P, NB, 2, EP], F16)
        xl_now = sb("xl_now", [P, 2, CJ, 2, EP], F16)
        ring = sb("ring", [P, 24 * 1024], U8)
        work = sb("work", [P, GB * 258], F32)
        comb = sb("comb", [P, GB, EP], F32)
        y = sb("y", [P, GB, D], F32)
        thr = sb("thr", [P, 2, GW], F32)
        masks = sb("masks", [P, 2, QG, HO, 2 * P], U8)
        step8 = sb("step8", [P, 8, GW], U8)
        ident = sb("ident", [P, P], F32)
        w_ea = sb("w_ea", [P, 3, EP], F32)
        a_col = sb("a_col", [P, 3, 2], F32)
        vec = {n: sb(f"v_{n}", [P, NB], F32) for n in (
            "mu", "rstd", "tmp", "tmp2", "s", "t", "keep", "v", "vl", "pow2", "mant", "clow",
            "lnc", "empty", "done", "new", "f", "z", "rest", "valid")}
        one = {n: sb(f"c_{n}", [P, 3], F32) for n in ("n2", "p2", "scale", "unscale", "knorm")}
        tm = sb("tm", [P, 2], F32)
        tmr = sb("tmr", [P, 2], F32)
        top = sb("top", [P, 1], F32)
        levels_f = sb("levels_f", [P, 1], F32)
        levels = sb("levels", [P, 3], I32)
        rows = sb("rows", [NB, 2, P], F32)
        vz = sb("vz", [P, NB, 10], BF16)
        stats8 = sb("stats8", [P, GB, 6], F32)
        vz_now = sb("vz_now", [P, 2, CJ, 10], BF16)
        psum = ctx.enter_context(nc.psum_tensor("psum", [P, 8, 512], F32))

        w_e, w_a = w_ea[:, :, 0:D], w_ea[:, :, D:EP]
        ones = y[:, 0, :]
        w_raw = comb[:, :, :].rearrange("p b w -> p (b w)")[:, 0:3 * D].rearrange("p (k d) -> p k d", k=3)
        tmp = work[:, 0:2 * GB * E].rearrange("p (s b w) -> p s b w", s=2, b=GB)
        stage = work[:, :].rearrange("p (b w) -> p b w", b=GB)
        zs = work[:, 0:NB * 10].rearrange("p (b w) -> p b w", b=NB)
        zr = work[:, NB * 10:NB * 13].rearrange("p (b w) -> p b w", b=NB)
        mean = vz[:, :, :].rearrange("p b w -> p (b w)").bitcast(F32)[:, 0:D]
        vec["var"] = vec["z"]
        vec["t_far"] = vec["empty"]
        stats = work[:, 0:NB * 6].rearrange("p (b w) -> p b w", b=NB)
        w_t = work[:, 1024:1024 + 3 * D].rearrange("p (k d) -> p k d", k=3)
        B8 = ring[:, 0:8192].rearrange("p (s w) -> p s w", s=RING)
        C8 = ring[:, 8192:16384].rearrange("p (s w) -> p s w", s=RING)
        B16 = ring[:, 16384:24576].bitcast(BF16).rearrange("p (s w) -> p s w", s=B16_RING)
        z_step = ring[:, 16384:24576].rearrange("p (s w) -> p s w", s=RING)
        planes8 = ring[:, 0:2 * N].rearrange("p (s k o w) -> p s k o w", s=2, k=8, o=OCT)
        packed8 = masks[:, :, :, :, :].rearrange("p s q o w -> p (s q o w)")[:, 0:2 * OCT * 2 * P].rearrange(
            "p (s o w) -> p s o w", s=2, o=OCT)
        bits = thr[:, :, :].rearrange("p s w -> p (s w)").bitcast(BF16)[:, 0:8 * P].rearrange("p (k w) -> p k w", k=8)
        hT = ring[:, 0:4096].bitcast(F32).rearrange("p (s w) -> p s w", s=2)
        hs = ring[:, 16384:20480].bitcast(F32).rearrange("p (s w) -> p s w", s=2)
        hr = ring[:, 20480:24576].bitcast(F32).rearrange("p (s w) -> p s w", s=2)
        adj_sb = e[:, :, :].rearrange("p b w -> p (b w)")[:, 0:NCOL * ADJ_COLS].bitcast(I32).rearrange("p (c w) -> p c w", c=NCOL)
        adj_bf = xl[:, :, :, :].rearrange("p a b c -> p (a b c)")[:, 0:NCOL * ADJ_COLS].bitcast(BF16).rearrange("p (c w) -> p c w", c=NCOL)

        def words4(ap):
            return ap.bitcast(U16).rearrange("p (q w) -> p q w", q=QG)

        def mask_words(half, o):
            return masks[:, half, :, bass.ds(o, 1), :].rearrange("p q a i -> p q (a i)").bitcast(U16)

        def two(tiles, slot):
            return tiles[:, slot:slot + 2, :].rearrange("p s w -> p (s w)").bitcast(U16)

        def pick(out, packed, k):
            both = (MASK << 8) | MASK
            if k <= 6:
                return nc.vector.tensor_scalar(out, packed, 6 - k, both, ALU.logical_shift_left, ALU.bitwise_and)
            return nc.vector.tensor_scalar(out, packed, 1, both, ALU.logical_shift_right, ALU.bitwise_and)

        def over(v, width):
            return v.unsqueeze(2).to_broadcast([P, v.shape[1], width])

        x_loaded, w_loaded, const_ready = sem("x_loaded"), sem("w_loaded"), sem("const_ready")
        w_trans, w_copied, w_proj, norm2_ready, w_norm, w_ready = (sem(n) for n in (
            "w_trans", "w_copied", "w_proj", "norm2_ready", "w_norm", "w_ready"))
        adj_loaded = [sem(f"adj_loaded{c}") for c in range(NCOL)]
        adj_masked, packed = sem("adj_masked"), sem("packed")
        evacuated = sem("evacuated")
        planes = sem("planes")
        sums_done = sem("sums_done")
        sums_read = sem("sums_read")
        mask_stored = [sem(f"mask_stored{s}") for s in range(2)]
        h_used = sem("h_used")
        ALL = (0,) + LAYERS
        var_ready, std_ready = sem("var_ready"), sem("std_ready")
        h_raw, h_ready = (per_layer(n, ALL) for n in ("h_raw", "h_ready"))
        hi_ready = sem("hi_ready")
        h_trans, hT_ready, e_made, e_ready = (per_layer(n) for n in ("h_trans", "hT_ready", "e_made", "e_ready"))
        t_range, t_range_all, levels_ready = (sem(n) for n in ("t_range", "t_range_all", "levels_ready"))
        neg_s, neg_s_trans, neg_s_row, neg_s_stored = (sem(n) for n in ("neg_s", "neg_s_trans", "neg_s_row", "neg_s_stored"))
        gaps_ready, exps_ready, scales_ready = (per_layer(n) for n in ("gaps_ready", "exps_ready", "scales_ready"))
        prod_ready, hi_done, parts_ready = (per_layer(n) for n in ("prod_ready", "hi_done", "parts_ready"))
        pe_gated, sp_gated = sem("pe_gated"), sem("sp_gated")
        thr_ready = per_layer("thr_ready")
        masks_ready = {l: [sem(f"masks_ready{l}_{s}") for s in range(2)] for l in LAYERS}
        unpacked = per_layer("unpacked")
        stepped, kept8 = per_layer("stepped"), sem("kept8")
        act_stepped = sem("act_stepped")
        upper8 = per_layer("upper8")
        lower8 = per_layer("lower8")
        upper16 = per_layer("upper16")
        xl_loaded = {l: [sem(f"xl_loaded{l}_{s}") for s in range(2)] for l in LAYERS}
        tile_done = per_layer("tile_done")
        bank_done = per_layer("bank_done")
        bank_read = per_layer("bank_read")
        stage_used = per_layer("stage_used")
        mean_added = sem("mean_added")
        z_parts, z_thr_ready, z_stepped, z_upper8, z_read = (sem(n) for n in (
            "z_parts", "z_thr_ready", "z_stepped", "z_upper8", "z_read"))
        z_columns, z_act_stepped = sem("z_columns"), sem("z_act_stepped")
        z_unpacked = sem("z_unpacked")
        z_tile = sem("z_tile")
        z_masks_ready = [sem(f"z_masks_ready{s}") for s in range(2)]
        row_sum, row_ln, cuts, cuts_trans, cut_rows, cut_stored = (sem(n) for n in (
            "row_sum", "row_ln", "cuts", "cuts_trans", "cut_rows", "cut_stored"))
        elu_neg, elu_exp = sem("elu_neg"), sem("elu_exp")
        x_final, x_stored = sem("x_final"), sem("x_stored")

        def n_levels(eng, l):
            eng.wait_ge(levels_ready, l)
            return eng.value_load(levels[0:1, l - 1:l], min_val=1, max_val=MAX_LEVELS)

        block = ctx.enter_context(nc.Block())

        @block.sync
        def _(sp):
            def gate():
                sp.nop().then_inc(sp_gated, 1)

            sp.dma_start(x[:, :, :], x_in.rearrange("(b p) d -> p b d", p=P)).then_inc(x_loaded, 16)
            for k, (w, a) in enumerate(((w1, a1), (w2, a2), (w3, a3))):
                sp.dma_start(w_raw[:, k, :], w).then_inc(w_loaded, 16)
                with nc.allow_non_contiguous_dma(reason="256 numbers"):
                    sp.dma_start(a_col[:, k, :], a.rearrange("(h p) o -> p (h o)", p=P)).then_inc(w_loaded, 16)

            adj_rows = adj_in.rearrange("(b p) (c w) -> c b p w", p=P, w=ADJ_COLS)
            for first in (True, False):
                with nullcontext(0) if first else sp.Fori(1, NB) as b:
                    for c in range(NCOL):
                        if not first:
                            sp.wait_ge(adj_masked, (b - 1) * NCOL + c + 1)
                        sp.dma_start(adj_sb[:, c, :], adj_rows[c, bass.ds(b, 1)].rearrange("a p w -> (a p) w")) \
                            .then_inc(adj_loaded[c], 16)

            def load_masks(ready, g, half):
                sp.dma_start(masks[:, half].rearrange("p q o i -> p q (o i)"),
                             mask_dram[bass.ds(g * QG, QG), :, half * HO:(half + 1) * HO, :].rearrange(
                                 "q p o i -> p q (o i)")).then_inc(ready[half], 16)

            def load_thr(l, which, row, g, ready):
                sp.dma_start(thr[:, which, :], row_dram[l][row, bass.ds(g * GB, GB), :].rearrange("b p -> (b p)")
                             .partition_broadcast(P)).then_inc(ready, 16)

            for l in LAYERS:
                sp.wait_ge(neg_s_row, l)
                sp.dma_start(row_dram[l][0, :, :], rows[:, 0, :]).then_inc(neg_s_stored, 16)
                sp.wait_ge(neg_s_stored, 16 * l)
                if l == 1:
                    for s in range(2):
                        sp.wait_ge(mask_stored[s], 16 * (NB // 4) + 16)
                n_lev = n_levels(sp, l)
                with sp.Fori(0, n_lev) as lev:
                    if l == 3:
                        sp.wait_ge(lower8[3], lev * TILES + 1)
                        gate()
                        with sp.Fori(0, G) as g:
                            for half in range(2):
                                sp.wait_ge(z_unpacked, lev * TILES + g * NB + (half + 1) * (NB // 2))
                                gate()
                                load_masks(z_masks_ready, g, half)
                                if half == 0:
                                    sp.wait_ge(z_stepped, (lev * G + g) * NBODY * Z_DVE + 1)
                                    sp.wait_ge(z_act_stepped, (lev * G + g) * NBODY * Z_ACT + 1)
                                    gate()
                                    load_thr(3, 0, 0, g, z_thr_ready)
                        sp.wait_ge(cut_rows, lev + 1)
                        gate()
                        sp.dma_start(row_dram[3][1:3, :, :].rearrange("r b p -> b r p"), rows[:, :, :]) \
                            .then_inc(cut_stored, 16)
                        sp.wait_ge(cut_stored, lev * 16 + 32)
                        gate()
                    with sp.Fori(0, G) as g:
                        for half in range(2):
                            sp.wait_ge(unpacked[l], lev * TILES + g * NB + (half + 1) * (NB // 2))
                            gate()
                            load_masks(masks_ready[l], g, half)
                            if half == 0:
                                sp.wait_ge(stepped[l], lev * TILES + g * NB + 1)
                                if l == 3:
                                    sp.wait_ge(act_stepped, (lev * G + g) * NBODY * N_ACT + 1)
                                gate()
                                if l == 3:
                                    load_thr(3, 0, 1, g, thr_ready[3])
                                    load_thr(3, 1, 2, g, thr_ready[3])
                                else:
                                    load_thr(l, 0, 0, g, thr_ready[l])
            sp.wait_ge(x_final, 1)
            sp.dma_start(x_out.rearrange("(b p) d -> p b d", p=P), x[:, :, :]).then_inc(x_stored, 16)
            sp.wait_ge(x_stored, 16)

        @block.gpsimd
        def _(pool):
            for s, n in ([(evacuated, 2), (planes, 32), (sums_done, 2), (sums_read, 2), (z_tile, RING), (z_stepped, 1),
                          (z_act_stepped, 1), (act_stepped, 1), (z_upper8, RING), (z_unpacked, NB), (z_read, 1),
                          (mask_stored[0], 16), (mask_stored[1], 16), (cut_stored, 16)]
                         + [(s, n) for l in LAYERS for s, n in (
                             (lower8[l], 1), (unpacked[l], NB), (upper8[l], 4), (upper16[l], RING), (tile_done[l], RING),
                             (bank_read[l], GB), (stage_used[l], 1), (stepped[l], 1))]):
                pool.nop().then_inc(s, n)
            nc.gpsimd.memset(ones[:, :], 1.0)
            nc.gpsimd.memset(ident[:, :], 0.0)
            pool.drain()
            nc.gpsimd.affine_select(out=ident[:, :], in_=ident[:, :], compare_op=ALU.not_equal, fill=1.0, base=0,
                                    pattern=[[-1, P]], channel_multiplier=1)
            pool.drain()
            for k in range(8):
                nc.gpsimd.tensor_scalar(bits[:, k, :], ident[:, :], float(1 << k), None, ALU.mult)
            nc.gpsimd.memset(xu[:, :, 0, NORM:NORM + 1], 1.0)
            nc.gpsimd.memset(xu[:, :, 1, NORM:NORM + 1], 0.0)
            nc.gpsimd.memset(xl[:, :, :, E:EP], 0.0)
            pool.drain().then_inc(const_ready, 1)

            for l in (1, 2):
                one_pass = lambda b: e[:, b * GB:(b + 1) * GB, 0:D]
                pool.wait_ge(t_range, l)
                nc.gpsimd.partition_all_reduce(tmr[:, :], tm[:, :], P, bass.bass_isa.ReduceOp.max) \
                    .then_inc(t_range_all, 1)
                pool.wait_ge(e_ready[l], NB // UB)
                nc.gpsimd.tensor_tensor(y[:, :, :], one_pass(0), one_pass(1), ALU.add)
                for b in range(2, NB // GB):
                    pool.drain()
                    nc.gpsimd.tensor_tensor(y[:, :, :], y[:, :, :], one_pass(b), ALU.add)
                half = GB // 2
                while half:
                    pool.drain()
                    nc.gpsimd.tensor_tensor(y[:, 0:half, :], y[:, 0:half, :], y[:, half:2 * half, :], ALU.add)
                    half //= 2
                pool.drain()
                nc.gpsimd.partition_all_reduce(mean[:, :], y[:, 0, :], P, bass.bass_isa.ReduceOp.add)
                pool.drain()
                nc.gpsimd.tensor_scalar(mean[:, :], mean[:, :], one["unscale"][:, l - 1:l], 1.0 / N, ALU.mult, ALU.mult)
                if l == 1:
                    pool.drain()
                    nc.gpsimd.tensor_scalar(mean[:, :], mean[:, :], 0.0, None, ALU.max)
                with pool.Fori(0, G) as g:
                    pool.drain()
                    nc.gpsimd.tensor_tensor(y[:, :, :], mean[:, :].unsqueeze(1).to_broadcast([P, GB, D]),
                                            over(vec["empty"][:, bass.ds(g * GB, GB)], D), ALU.mult)
                    pool.drain()
                    nc.gpsimd.tensor_tensor(x[:, bass.ds(g * GB, GB), :], x[:, bass.ds(g * GB, GB), :], y[:, :, :], ALU.add)
                pool.drain().then_inc(mean_added, 1)
            pool.wait_ge(t_range, 3)
            nc.gpsimd.partition_all_reduce(tmr[:, :], tm[:, :], P, bass.bass_isa.ReduceOp.max) \
                .then_inc(t_range_all, 1)

        @block.tensor
        def _(pe):
            def gate():
                pe.nop().then_inc(pe_gated, 1)

            pe.wait_ge(w_loaded, 16 * 6)
            pe.wait_ge(const_ready, 1)
            for k in range(3):
                mm = nc.tensor.transpose(psum[:, 5, k * P:(k + 1) * P], w_raw[:, k, :], ident[:, :])
            mm.then_inc(w_trans, 1)
            pe.wait_ge(w_copied, 1)
            for k in range(3):
                w_out_in = w_raw[:, k, :] if k == 0 else w_t[:, k, :]
                mm = nc.tensor.matmul(psum[:, 6, 2 * k:2 * k + 2], w_out_in, a_col[:, k, :], start=True, stop=True)
                mm = nc.tensor.matmul(psum[:, 7, k * P:(k + 1) * P], ones[:, :], w_e[:, k, :], start=True, stop=True)
            mm.then_inc(w_proj, 1)

            def pack(b, slot, c):
                pe.wait_ge(adj_masked, b * NCOL + c + 1)
                if c == 0:
                    pe.wait_ge(evacuated, b + 1)
                for o in (2 * c, 2 * c + 1):
                    for k in range(8):
                        at = (8 * (o % 2) + k) * P
                        mm = nc.tensor.matmul(psum[:, 2 * slot + o // 4, o % 4 * P:(o % 4 + 1) * P],
                                              adj_bf[:, c, at:at + P], bits[:, k, :],
                                              start=(o % 4 == 0 and k == 0), stop=True, skip_group_check=True)
                mm.then_inc(packed, 1)

            def sums(b, slot, c):
                if c == 0:
                    pe.wait_ge(sums_read, b + 1)
                pe.wait_ge(planes, 8 * b + (c + 1) * PLANES + 32)
                gate()
                for k in range(c * PLANES, (c + 1) * PLANES):
                    for o in range(OCT):
                        for part in range(2):
                            mm = nc.tensor.matmul(psum[:, 4 + slot, 0:E], planes8[:, slot, k, o, :].bitcast(F8),
                                                  xu[:, 8 * o + k, part, 0:E], start=(k == 0 and o == 0 and part == 0),
                                                  stop=(k == 7 and o == OCT - 1 and part == 1), skip_group_check=True)
                if c == NCOL - 1:
                    mm.then_inc(sums_done, 1)

            pe.wait_ge(w_norm, 1)
            for b in range(LEAD):
                for c in range(NCOL):
                    pack(b, b % 2, c)
            pe.wait_ge(h_used, NB // UB)
            with pe.Fori(0, (NB - 4) // 2) as i:
                for u in range(2):
                    for c in range(NCOL):
                        pack(2 * i + u + LEAD, (u + LEAD) % 2, c)
                        sums(2 * i + u, u, c)
            for b in range(NB - 4, NB):
                for c in range(NCOL):
                    if b + LEAD < NB:
                        pack(b + LEAD, (b + LEAD) % 2, c)
                    sums(b, b % 2, c)

            for l in LAYERS:
                k_w = l - 1
                if l == 1:
                    pe.wait_ge(w_ready, 1)

                def transpose_h(unit, s, first):
                    pe.wait_ge(h_ready[l], unit + 1)
                    if not first:
                        pe.wait_ge(hT_ready[l], unit - 1)
                    for k in range(UB):
                        mm = nc.tensor.transpose(psum[:, s, k * P:(k + 1) * P], hr[:, s, k * P:(k + 1) * P], ident[:, :])
                    mm.then_inc(h_trans[l], 1)

                def project(unit, s, first):
                    pe.wait_ge(hT_ready[l], unit + 1)
                    if not first:
                        pe.wait_ge(e_ready[l], unit - 1)
                    for k in range(UB):
                        mm = nc.tensor.matmul(psum[:, 2 + 2 * s + k // 2, k % 2 * EP:(k % 2 + 1) * EP],
                                              hT[:, s, k * P:(k + 1) * P], w_ea[:, k_w, :], start=True, stop=True)
                    mm.then_inc(e_made[l], 1)

                NU = NB // UB
                for u in range(2):
                    transpose_h(u, u, True)
                for u in range(2):
                    project(u, u, True)
                    transpose_h(u + 2, u, False)
                with pe.Fori(1, NU // 2 - 1) as i:
                    for u in range(2):
                        project(2 * i + u, u, False)
                        transpose_h(2 * i + u + 2, u, False)
                for u in range(2):
                    project(NU - 2 + u, u, False)
                pe.wait_ge(neg_s, l)
                nc.tensor.transpose(psum[0:NB, 5, 0:P], vec["tmp"][:, :], ident[:, :]).then_inc(neg_s_trans, 1)

                n_lev = n_levels(pe, l)
                with pe.Fori(0, n_lev) as lev:
                    if l == 3:
                        pe.wait_ge(z_parts, lev + 1)
                        gate()
                        with pe.Fori(0, G) as g:
                            pe.wait_ge(z_read, lev * G + g + 1)
                            for first in (True, False):
                                with nullcontext(0) if first else pe.Fori(1, NBODY) as c:
                                    for u in range(BODY):
                                        n = lev * TILES + g * NB + c * BODY + u
                                        pe.wait_ge(z_upper8, n + 1 + RING)
                                        if u % CJ == 0:
                                            pe.wait_ge(z_columns, lev * (TILES // CJ) + g * (NB // CJ) + c * 2 + u // CJ + 1)
                                        gate()
                                        for b in range(GB):
                                            nc.tensor.matmul(psum[:, b, 0:6], B8[:, u, b * P:(b + 1) * P].bitcast(F8),
                                                             vz_now[:, u // CJ, u % CJ, 0:6],
                                                             start=(first and u == 0), stop=True, skip_group_check=True)
                                            mm = nc.tensor.matmul(psum[:, b, 6:10],
                                                                  C8[:, u, b * P:(b + 1) * P].bitcast(F8),
                                                                  vz_now[:, u // CJ, u % CJ, 6:10],
                                                                  start=False, stop=True, skip_group_check=True)
                                        mm.then_inc(z_tile, 1)
                        pe.wait_ge(cuts, lev + 1)
                        gate()
                        nc.tensor.transpose(psum[0:NB, 0, 0:P], vec["tmp"][:, :], ident[:, :])
                        nc.tensor.transpose(psum[0:NB, 0, P:2 * P], vec["tmp2"][:, :], ident[:, :]).then_inc(cuts_trans, 1)
                        pe.wait_ge(cut_rows, lev + 1)
                        gate()
                    with pe.Fori(0, G) as g:
                        for first in (True, False):
                            with nullcontext(0) if first else pe.Fori(1, NBODY) as c:
                                pe.wait_ge(parts_ready[l], lev * NBODY + c + 1)
                                for u in range(BODY):
                                    n = lev * TILES + g * NB + c * BODY + u
                                    pe.wait_ge(lower8[l], n + 2)
                                    if u % CJ == 0:
                                        pe.wait_ge(xl_loaded[l][u // CJ], 16 * (lev * G * NBODY + g * NBODY + c + 1))
                                    pe.wait_ge(upper16[l], n + 1 + RING)
                                    for b in range(GB):
                                        if first and u == 0:
                                            pe.wait_ge(bank_read[l], lev * NB + g * GB + b + 1)
                                        for part in range(2):
                                            mm = nc.tensor.matmul(
                                                psum[:, b, 0:E], B16[:, u % B16_RING, b * P:(b + 1) * P],
                                                xu[:, bass.ds(c * BODY + u, 1), part, 0:E].rearrange("p a w -> p (a w)"),
                                                start=(first and u == 0 and part == 0), stop=True, skip_group_check=True)
                                        for part in range(2):
                                            mm = nc.tensor.matmul(
                                                psum[:, b, E:2 * E], C8[:, u, b * P:(b + 1) * P].bitcast(F8),
                                                xl_now[:, u // CJ, u % CJ, part, 0:E],
                                                start=False, stop=True, skip_group_check=True)
                                        if u == BODY - 1 and b < GB - 1:
                                            mm.then_inc(bank_done[l], 1)
                                    mm.then_inc(tile_done[l], 1)

        @block.scalar
        def _(act):
            act.wait_ge(norm2_ready, 1)
            nc.scalar.activation(one["n2"][:, :], one["n2"][:, :], ACT.Sqrt).then_inc(w_norm, 1)

            def normalise(l):
                act.wait_ge(var_ready, l + 1)
                nc.scalar.activation(vec["rstd"][:, :], vec["var"][:, :], ACT.Sqrt).then_inc(std_ready, 1)

            def relu(l, unit, s, first):
                act.wait_ge(h_raw[l], unit + 1)
                if not first:
                    act.wait_ge(h_used if l == 0 else h_trans[l], unit - 1)
                nc.scalar.activation(hr[:, s, :], hs[:, s, :], ACT.Relu).then_inc(h_ready[l], 1)

            def blocks(s):
                return hr[:, s, :].rearrange("p (b d) -> p b d", b=UB)

            def evacuate(b, u):
                slot = u // 2
                act.wait_ge(packed, (b + 1) * NCOL)
                act.wait_ge(planes, 8 * b + 8)
                nc.scalar.activation(packed8[:, slot, :, u % 2 * P:(u % 2 + 1) * P],
                                     psum[:, 2 * (u % 2):2 * (u % 2) + 2, :].rearrange("p k (o w) -> p (k o) w", w=P)
                                     [:, 0:OCT, :], ACT.Copy).then_inc(evacuated, 1)

            def store(pair, slot, b):
                act.wait_ge(evacuated, b + 1 + 2)
                act.dma_start(mask_dram[bass.ds(pair, 1)].rearrange("a p o i -> p (a o) i"), packed8[:, slot]) \
                    .then_inc(mask_stored[slot], 16)

            def stored_before(slot, count):
                act.wait_ge(mask_stored[slot], 16 * count + 16)

            normalise(0)
            QUARTER = NB // UB // 4 // 2
            for quarter in range(4):
                for first in (True, False) if quarter == 0 else (False,):
                    lo, hi_ = quarter * QUARTER + (quarter == 0), (quarter + 1) * QUARTER
                    if not first and lo == hi_:
                        continue
                    with nullcontext(0) if first else act.Fori(lo, hi_) as i:
                        for s in range(2):
                            unit = 2 * i + s
                            relu(0, unit, s, first)
                            act.wait_ge(h_ready[0], unit + 1)
                            nc.scalar.activation(xu[:, bass.ds(unit * UB, UB), 0, 0:D], blocks(s), ACT.Copy,
                                                 scale=H_SCALE).then_inc(hi_ready, 1)
                if quarter < LEAD:
                    evacuate(quarter, quarter)
                    if quarter == 1:
                        store(0, 0, 1)

            with act.Fori(0, (NB - 4) // 4) as i:
                evacuate(4 * i + 3, 3)
                store(2 * i + 1, 1, 4 * i + 3)
                stored_before(0, i + 1)
                evacuate(4 * i + 4, 0)
                evacuate(4 * i + 5, 1)
                store(2 * i + 2, 0, 4 * i + 5)
                stored_before(1, i + 1)
                evacuate(4 * i + 6, 2)
            evacuate(NB - 1, 3)
            store(NB // 2 - 1, 1, NB - 1)

            for l in LAYERS:
                slope = SLOPE[l]
                normalise(l)

                def e_out(unit, s):
                    act.wait_ge(e_made[l], unit + 1)
                    nc.scalar.activation(e[:, bass.ds(unit * UB, UB), :].rearrange("p (k b) w -> p k (b w)", k=2),
                                         psum[:, 2 + 2 * s:4 + 2 * s, 0:2 * EP], ACT.Copy) \
                        .then_inc(e_ready[l], 1)

                NU = NB // UB
                for u in range(2):
                    relu(l, u, u, True)
                with act.Fori(0, NU // 2 - 1) as i:
                    for u in range(2):
                        relu(l, 2 * i + u + 2, u, False)
                        e_out(2 * i + u, u)
                for u in range(2):
                    e_out(NU - 2 + u, u)

                n_lev = n_levels(act, l)
                with act.Fori(0, n_lev) as lev:
                    act.wait_ge(gaps_ready[l], lev + 1)
                    nc.scalar.activation(vec["v"][:, :], vec["tmp2"][:, :], ACT.Exp)
                    nc.scalar.activation(vec["vl"][:, :], vec["tmp2"][:, :], ACT.Exp, scale=slope)
                    nc.scalar.activation(vec["clow"][:, :], vec["lnc"][:, :], ACT.Exp).then_inc(exps_ready[l], 1)

                    if l == 3:
                        def z_columns_of(g, c, k):
                            act.wait_ge(z_tile, lev * TILES + g * NB + c * BODY + (k + 1) * CJ)
                            nc.scalar.activation(vz_now[:, k, :, :], vz[:, bass.ds(c * BODY + k * CJ, CJ), :],
                                                 ACT.Copy).then_inc(z_columns, 1)

                        def z_steps(g, c, tiles):
                            for u in tiles:
                                act.wait_ge(z_upper8, lev * TILES + g * NB + c * BODY + u + 1)
                                nc.scalar.activation(z_step[:, u, :], thr[:, 0, :], ACT.Relu,
                                                     bias=vec["t_far"][:, bass.ds(c * BODY + u, 1)], scale=-FAR) \
                                    .then_inc(z_act_stepped, 1)

                        act.wait_ge(z_parts, lev + 1)
                        with act.Fori(0, G) as g:
                            act.wait_ge(z_thr_ready, 16 * (lev * G + g + 1))
                            for first in (True, False):
                                with nullcontext(0) if first else act.Fori(1, NBODY) as c:
                                    z_steps(g, c, range(0, 2))
                                    z_columns_of(g, c, 0)
                                    z_steps(g, c, range(2, 4))
                                    z_columns_of(g, c, 1)
                                    z_steps(g, c, range(4, Z_ACT))
                            act.wait_ge(z_tile, lev * TILES + (g + 1) * NB + RING)
                            nc.scalar.activation(zs[:, bass.ds(g * GB, GB), :], psum[:, :, 0:10], ACT.Copy).then_inc(z_read, 1)
                        act.wait_ge(row_sum, lev + 1)
                        nc.scalar.activation(vec["z"][:, :], vec["z"][:, :], ACT.Ln).then_inc(row_ln, 1)

                    def hi(c):
                        for k, half in enumerate((xu, xl)):
                            act.wait_ge(prod_ready[l], lev * 2 * NBODY + 2 * c + k + 1)
                            nc.scalar.activation(half[:, bass.ds(c * GB, GB), 0, 0:E], tmp[:, k, :, :], ACT.Copy) \
                                .then_inc(hi_done[l], 1)

                    def split(g, c, u):
                        if u % BODY < N_ACT:
                            act.wait_ge(upper8[3], lev * TILES + g * NB + c * BODY + u + 1)
                            nc.scalar.activation(step8[:, u % 4, :], thr[:, 0, :], ACT.Relu,
                                                 bias=vec["t_far"][:, bass.ds(c * BODY + u, 1)], scale=-FAR) \
                                .then_inc(act_stepped, 1)

                    def scale_upper(g, c, tiles, opening=False, closing=False):
                        for u in tiles:
                            n = lev * TILES + g * NB + c * BODY + u
                            if u % CJ == 0:
                                act.wait_ge(tile_done[l], n - CJ + RING)
                                act.dma_start(xl_now[:, u // CJ], xl[:, bass.ds(c * BODY + u, CJ)]) \
                                    .then_inc(xl_loaded[l][u // CJ], 16)
                            if l == 3 and u % 2 == 0:
                                for ahead in range(0 if u == 0 and opening else u + 2, u + 4):
                                    if ahead < BODY or not closing:
                                        split(g, c, ahead)
                            act.wait_ge(upper8[l], n + 1 + 4)
                            act.wait_ge(tile_done[l], n + 1 + RING - B16_RING)
                            nc.scalar.activation(B16[:, u % B16_RING, :], B8[:, u, :], ACT.Copy,
                                                 scale=vec["pow2"][:, bass.ds(c * BODY + u, 1)]).then_inc(upper16[l], 1)

                    def read_banks(g):
                        act.wait_ge(stage_used[l], lev * G + g + 1)
                        for b in range(GB):
                            if b < GB - 1:
                                act.wait_ge(bank_done[l], (GB - 1) * (lev * G * NBODY + (g + 1) * NBODY - 1) + b + 1)
                            else:
                                act.wait_ge(tile_done[l], lev * TILES + (g + 1) * NB + RING)
                            nc.scalar.activation(stage[:, b, :], psum[:, b, 0:2 * E], ACT.Copy).then_inc(bank_read[l], 1)

                    def elu(g):
                        act.wait_ge(elu_neg, lev * G + g + 1)
                        nc.scalar.activation(comb[:, :, 0:D], comb[:, :, 0:D], ACT.Exp).then_inc(elu_exp, 1)

                    act.wait_ge(scales_ready[l], lev + 1)
                    if l == 3:
                        act.wait_ge(thr_ready[3], 32 * (lev * G + 1))
                    def first_group(c, **ends):
                        hi(c)
                        act.wait_ge(parts_ready[l], lev * NBODY + c + 1)
                        scale_upper(0, c, range(BODY), **ends)

                    first_group(0, opening=True)
                    with act.Fori(1, NBODY - 1) as c:
                        first_group(c)
                    first_group(NBODY - 1, closing=True)
                    with act.Fori(1, G) as g:
                        if l == 3:
                            act.wait_ge(thr_ready[3], 32 * (lev * G + g + 1))
                        scale_upper(g, 0, range(B16_RING - 1), opening=True)
                        read_banks(g - 1)
                        scale_upper(g, 0, range(B16_RING - 1, BODY))
                        if l == 3:
                            elu(g - 1)
                        with act.Fori(1, NBODY - 1) as c:
                            scale_upper(g, c, range(BODY))
                        scale_upper(g, NBODY - 1, range(BODY), closing=True)
                    read_banks(G - 1)
                    if l == 3:
                        elu(G - 1)

        @block.vector
        def _(dve):
            ve = nc.vector
            dve.wait_ge(w_loaded, 16 * 6)
            dve.wait_ge(w_trans, 1)
            ve.tensor_copy(w_t[:, :, :], psum[:, 5, 0:3 * P].rearrange("p (k d) -> p k d", k=3))
            dve.drain()
            in_out = [w_t[:, 0, :], w_raw[:, 1, :], w_raw[:, 2, :]]
            for k in range(3):
                ve.tensor_tensor(w_e[:, k, :], in_out[k], in_out[k], ALU.mult)
            dve.drain().then_inc(w_copied, 1)
            dve.wait_ge(w_proj, 1)
            ve.tensor_copy(w_a[:, :, :], psum[:, 6, 0:6].rearrange("p (k d) -> p k d", k=3))
            ve.tensor_reduce(one["n2"][:, :], psum[:, 7, 0:3 * P].rearrange("p (k d) -> p k d", k=3), AX_X, ALU.max)
            dve.drain().then_inc(norm2_ready, 1)
            dve.wait_ge(w_norm, 1)
            ve.tensor_scalar(one["n2"][:, :], one["n2"][:, :], LEAST, None, ALU.max)
            dve.drain()
            ve.tensor_scalar(one["p2"][:, :].bitcast(I32), one["n2"][:, :].bitcast(I32), EXP_BITS, None, ALU.bitwise_and)
            dve.drain()
            ve.tensor_scalar(one["unscale"][:, :], one["p2"][:, :], 1.0 / E_BOUND, None, ALU.mult)
            dve.drain()
            ve.reciprocal(one["scale"][:, :], one["unscale"][:, :])
            ve.tensor_scalar(one["knorm"][:, :], one["unscale"][:, :], NORM_SCALE, None, ALU.mult)
            dve.drain()
            for k in range(3):
                ve.tensor_scalar(w_e[:, k, :], in_out[k], one["scale"][:, k:k + 1], None, ALU.mult)
            dve.drain().then_inc(w_ready, 1)

            def fold(parts, mu, var):
                m0, q0, m1, q1 = (parts[:, :, k] for k in (1, 2, 4, 5))
                d, q = parts[:, :, 0], parts[:, :, 3]
                dve.drain()
                ve.tensor_tensor(mu, m0, m1, ALU.add)
                ve.tensor_tensor(d, m0, m1, ALU.subtract)
                ve.tensor_tensor(q, q0, q1, ALU.add)
                dve.drain()
                ve.tensor_scalar(mu, mu, 0.5, None, ALU.mult)
                ve.tensor_tensor(d, d, d, ALU.mult)
                dve.drain()
                ve.scalar_tensor_tensor(out=q, in0=d, scalar=D / 4.0, in1=q, op0=ALU.mult, op1=ALU.add)
                dve.drain()
                ve.tensor_scalar(var, q, 1.0 / D, EPS, ALU.mult, ALU.add)

            def deviations(l):
                dve.drain().then_inc(var_ready, 1)
                dve.wait_ge(std_ready, l + 1)
                ve.reciprocal(vec["rstd"][:, :], vec["rstd"][:, :])
                dve.drain()

            def centre(l, unit, s, first):
                if not first:
                    dve.wait_ge(h_ready[l], unit - 1)
                for k in range(UB):
                    b = unit * UB + k
                    out = ve.tensor_scalar(hs[:, s, k * P:(k + 1) * P], x[:, bass.ds(b, 1), :].rearrange("p a w -> p (a w)"),
                                           vec["mu"][:, bass.ds(b, 1)], vec["rstd"][:, bass.ds(b, 1)],
                                           ALU.subtract, ALU.mult)
                out.then_inc(h_raw[l], 1)

            def make_mask(b, c, first=False):
                dve.wait_ge(adj_loaded[c], 16 * b + 16)
                if not first:
                    dve.wait_ge(packed, (b - 1) * NCOL + c + 1)
                ve.tensor_scalar(adj_bf[:, c, :], adj_sb[:, c, :], 0.0, None, ALU.is_gt).then_inc(adj_masked, 1)

            dve.wait_ge(x_loaded, 16)
            with dve.Fori(0, NB // 8) as i:
                for k in range(8):
                    ve.bn_stats(stats[:, bass.ds(i * 8 + k, 1), :].rearrange("p a w -> p (a w)"),
                                x[:, bass.ds(i * 8 + k, 1), :].rearrange("p a w -> p (a w)"))
            fold(stats, vec["mu"][:, :], vec["var"][:, :])
            deviations(0)
            dve.wait_ge(const_ready, 1)
            QUARTER = NB // UB // 4 // 2
            for quarter in range(4):
                for c in range(NCOL):
                    make_mask(quarter, c, first=(quarter == 0))
                for first in (True, False) if quarter == 0 else (False,):
                    lo, hi_ = quarter * QUARTER + (quarter == 0), (quarter + 1) * QUARTER
                    if not first and lo == hi_:
                        continue
                    with nullcontext(0) if first else dve.Fori(lo, hi_) as i:
                        for s in range(2):
                            centre(0, 2 * i + s, s, first)
                        for s in range(2):
                            unit = 2 * i + s
                            dve.wait_ge(hi_ready, unit + 1)
                            hb = hr[:, s, :].rearrange("p (b d) -> p b d", b=UB)
                            at = bass.ds(unit * UB, UB)
                            ve.scalar_tensor_tensor(out=xu[:, at, 1, 0:D], in0=hb, scalar=H_SCALE, in1=xu[:, at, 0, 0:D],
                                                    op0=ALU.mult, op1=ALU.subtract)
                            ve.tensor_tensor(x[:, at, :], x[:, at, :], hb, ALU.add).then_inc(h_used, 1)

            def unpack(b, u, slot):
                dve.wait_ge(evacuated, b + 1 + 2)
                dve.wait_ge(sums_done, b + 1)
                for k in range(8):
                    pick(planes8[:, slot, k].bitcast(U16), packed8[:, u // 2, :, u % 2 * P:(u % 2 + 1) * P].bitcast(U16),
                         k).then_inc(planes, 1)

            def add_sums(b, slot, b_mod):
                dve.wait_ge(sums_done, b + 1 + 2)
                at = bass.ds(b, 1)
                xb = x[:, at, :].rearrange("p a w -> p (a w)")
                ve.scalar_tensor_tensor(out=xb, in0=psum[:, 4 + slot, 0:D], scalar=1.0 / (H_SCALE * MASK_F8),
                                        in1=xb, op0=ALU.mult, op1=ALU.add)
                ve.tensor_scalar(vec["empty"][:, at], psum[:, 4 + slot, NORM:NORM + 1], 0.0, None,
                                 ALU.is_equal).then_inc(sums_read, 1)
                dve.drain()
                ve.bn_stats(stats8[:, b_mod, :], xb)
                if b_mod == 3:
                    at = bass.ds(b - 3, 4)
                    fold(stats8[:, 0:4, :], vec["mu"][:, at], vec["var"][:, at])
                    dve.drain()

            for b in range(2):
                unpack(b, b, b)
            with dve.Fori(0, (NB - 4) // 4) as i:
                for u in range(4):
                    for c in range(NCOL):
                        make_mask(4 * i + u + 4, c)
                    add_sums(4 * i + u, u % 2, u)
                    unpack(4 * i + u + 2, (u + 2) % 4, u % 2)
            for u in range(4):
                add_sums(NB - 4 + u, u % 2, u)
                if u < 2:
                    unpack(NB - 2 + u, u + 2, u % 2)
            dve.drain()

            def first_pass(lev):
                v3 = [(vec["v"], vz[:, :, 0:3]), (vec["vl"], vz[:, :, 3:6])]
                for value, parts in v3:
                    ve.tensor_copy(parts[:, :, 0], value[:, :])
                    dve.drain()
                    ve.tensor_tensor(vec["rest"][:, :], value[:, :], parts[:, :, 0], ALU.subtract)
                    dve.drain()
                    ve.tensor_copy(parts[:, :, 1], vec["rest"][:, :])
                    dve.drain()
                    ve.tensor_tensor(vec["rest"][:, :], vec["rest"][:, :], parts[:, :, 1], ALU.subtract)
                    dve.drain()
                    ve.tensor_copy(parts[:, :, 2], vec["rest"][:, :])
                    dve.drain()
                ve.tensor_copy(vz[:, :, 6:9], vz[:, :, 3:6])
                ve.tensor_copy(vz[:, :, 9], vec["valid"][:, :])
                dve.drain().then_inc(z_parts, 1)

                def cut_upper(g, half, o, new_group):
                    c = half * HO + o
                    if new_group:
                        dve.wait_ge(z_thr_ready, 16 * (lev * G + g + 1))
                    dve.wait_ge(z_masks_ready[half], 16 * (lev * G + g + 1))
                    body, first = (lev * G + g) * NBODY + c, lev * TILES + g * NB + c * BODY

                    def unpack_pair(u0):
                        dve.wait_ge(z_tile, first + u0 + 2)
                        for u in (u0, u0 + 1):
                            pick(words4(C8[:, u, :]), mask_words(half, o), u).then_inc(z_unpacked, 1)

                    unpack_pair(0)
                    for u0 in range(0, BODY, 2):
                        n0 = first + u0
                        for u in (u0, u0 + 1):
                            if u >= Z_ACT:
                                dve.wait_ge(z_upper8, n0 + (u - u0) + 1)
                                ve.tensor_scalar(z_step[:, u, :], thr[:, 0, :], vec["t"][:, bass.ds(c * BODY + u, 1)],
                                                 float(MASK), ALU.is_le, ALU.mult).then_inc(z_stepped, 1)
                        if u0 + 2 < BODY:
                            unpack_pair(u0 + 2)
                        dve.wait_ge(z_unpacked, n0 + 2 + NB)
                        if u0 < Z_ACT:
                            dve.wait_ge(z_act_stepped, body * Z_ACT + min(u0 + 2, Z_ACT) + 1)
                        if u0 + 1 >= Z_ACT:
                            dve.wait_ge(z_stepped, body * Z_DVE + u0 + 2 - Z_ACT + 1)
                        ve.tensor_tensor(two(B8, u0), two(z_step, u0), two(C8, u0), ALU.bitwise_and).then_inc(z_upper8, 2)

                with dve.Fori(0, G) as g:
                    cut_upper(g, 0, 0, True)
                    with dve.Fori(1, HO) as o:
                        cut_upper(g, 0, o, False)
                    with dve.Fori(0, HO) as o:
                        cut_upper(g, 1, o, False)

                dve.wait_ge(z_read, lev * G + G + 1)
                ve.tensor_reduce(zr[:, :, :], zs[:, :, 0:9].rearrange("p b (k w) -> p b k w", w=3), AX_X, ALU.add)
                dve.drain()
                ve.tensor_tensor(vec["rest"][:, :], zr[:, :, 2], zr[:, :, 1], ALU.subtract)
                dve.drain()
                ve.tensor_tensor(vec["rest"][:, :], vec["rest"][:, :], vec["clow"][:, :], ALU.mult)
                dve.drain()
                ve.scalar_tensor_tensor(out=vec["rest"][:, :], in0=zr[:, :, 0], scalar=1.0 / MASK_F8,
                                        in1=vec["rest"][:, :], op0=ALU.mult, op1=ALU.add)
                dve.drain()
                ve.tensor_scalar(vec["z"][:, :], vec["rest"][:, :], ROW_SUM_LEAST, None, ALU.max)
                ve.tensor_scalar(vec["new"][:, :], vec["rest"][:, :], ROW_SEEN[3], None, ALU.is_ge)
                ve.tensor_scalar(vec["tmp"][:, :], zs[:, :, 9], 0.0, None, ALU.is_equal)
                dve.drain()
                ve.reciprocal(vec["f"][:, :], vec["z"][:, :])
                ve.tensor_tensor(vec["new"][:, :], vec["new"][:, :], vec["tmp"][:, :], ALU.max)
                dve.drain().then_inc(row_sum, 1)
                ve.tensor_tensor(vec["new"][:, :], vec["new"][:, :], vec["done"][:, :], ALU.is_gt)
                ve.tensor_tensor(vec["f"][:, :], vec["f"][:, :], zs[:, :, 9], ALU.mult)
                dve.drain()
                ve.tensor_tensor(vec["done"][:, :], vec["done"][:, :], vec["new"][:, :], ALU.max)
                ve.tensor_scalar(vec["f"][:, :], vec["f"][:, :], one["unscale"][:, 2:3], 1.0 / MASK_F8, ALU.mult, ALU.mult)
                dve.drain()
                ve.tensor_tensor(vec["f"][:, :], vec["f"][:, :], vec["new"][:, :], ALU.mult)
                dve.wait_ge(row_ln, lev + 1)
                ve.tensor_scalar(vec["z"][:, :], vec["z"][:, :], float(np.log(THR)), None, ALU.add)
                dve.drain()
                ve.tensor_tensor(vec["rest"][:, :], vec["z"][:, :], vec["lnc"][:, :], ALU.subtract)
                ve.tensor_scalar(vec["tmp"][:, :], vec["z"][:, :], top[:, 0:1], None, ALU.add)
                dve.drain()
                ve.tensor_scalar(vec["rest"][:, :], vec["rest"][:, :], 1.0 / SLOPE[3], top[:, 0:1], ALU.mult, ALU.add)
                ve.scalar_tensor_tensor(out=vec["tmp"][:, :], in0=vec["s"][:, :], scalar=-1.0, in1=vec["tmp"][:, :],
                                        op0=ALU.mult, op1=ALU.max)
                dve.drain()
                ve.tensor_tensor(vec["tmp2"][:, :], vec["rest"][:, :], vec["tmp"][:, :], ALU.min)
                dve.drain().then_inc(cuts, 1)
                dve.wait_ge(cuts_trans, lev + 1)
                dve.wait_ge(cut_stored, 16 * lev + 16)
                ve.tensor_copy(rows[:, :, :], psum[0:NB, 0, 0:2 * P].rearrange("b (k p) -> b k p", k=2)).then_inc(cut_rows, 1)

            for l in LAYERS:
                slope, kw = SLOPE[l], l - 1
                deviations(l)
                if l == 1:
                    for s in range(2):
                        dve.wait_ge(mask_stored[s], 16 * (NB // 4) + 16)
                NU = NB // UB

                def copy_hT(unit, s, first):
                    dve.wait_ge(h_trans[l], unit + 1)
                    if not first:
                        dve.wait_ge(e_made[l], unit - 1)
                    ve.tensor_copy(hT[:, s, :], psum[:, s, :]).then_inc(hT_ready[l], 1)

                for u in range(2):
                    centre(l, u, u, True)
                for u in range(2):
                    centre(l, u + 2, u, False)
                    copy_hT(u, u, True)
                with dve.Fori(1, NU // 2 - 1) as i:
                    for u in range(2):
                        centre(l, 2 * i + u + 2, u, False)
                        copy_hT(2 * i + u, u, False)
                for u in range(2):
                    copy_hT(NU - 2 + u, u, False)

                dve.wait_ge(e_ready[l], NU)
                st = e[:, :, D:EP]
                ve.tensor_copy(vec["s"][:, :], st[:, :, 0])
                ve.tensor_copy(vec["t"][:, :], st[:, :, 1])
                ve.tensor_scalar(vec["tmp"][:, :], st[:, :, 0], -1.0, None, ALU.mult)
                ve.tensor_scalar(vec["tmp2"][:, :], st[:, :, 1], -1.0, None, ALU.mult)
                dve.drain().then_inc(neg_s, 1)
                ve.tensor_reduce(tm[:, 0:1], vec["t"][:, :], AX_X, ALU.max)
                ve.tensor_reduce(tm[:, 1:2], vec["tmp2"][:, :], AX_X, ALU.max)
                dve.drain().then_inc(t_range, 1)
                ve.memset(vec["done"][:, :], 0.0)
                ve.memset(e[:, :, NORM:NORM + 1], NORM_SCALE)
                if l == 3:
                    ve.tensor_scalar(vec["t_far"][:, :], vec["t"][:, :], FAR, None, ALU.mult)
                dve.wait_ge(neg_s_trans, l)
                ve.tensor_copy(rows[:, 0, :], psum[0:NB, 5, 0:P]).then_inc(neg_s_row, 1)
                if l == 3:
                    ve.tensor_reduce(vec["valid"][:, :], e[:, :, 0:D], AX_X, ALU.add)
                    dve.drain()
                    ve.tensor_scalar(vec["valid"][:, :], vec["valid"][:, :], 0.0, None, ALU.not_equal)
                dve.wait_ge(t_range_all, l)
                ve.tensor_copy(top[:, :], tmr[:, 0:1])
                ve.tensor_tensor(levels_f[:, :], tmr[:, 0:1], tmr[:, 1:2], ALU.add)
                dve.drain()
                ve.tensor_scalar(levels_f[:, :], levels_f[:, :], 1.0 / WINDOW[l], 1.0, ALU.mult, ALU.add)
                dve.drain()
                ve.tensor_scalar(levels_f[:, :], levels_f[:, :], float(MAX_LEVELS), None, ALU.min)
                dve.drain()
                ve.tensor_copy(levels[:, kw:kw + 1], levels_f[:, :])
                dve.drain().then_inc(levels_ready, 1)

                n_lev = n_levels(dve, l)
                with dve.Fori(0, n_lev) as lev:
                    ve.tensor_scalar(vec["tmp2"][:, :], vec["t"][:, :], top[:, 0:1], None, ALU.subtract)
                    ve.tensor_scalar(vec["lnc"][:, :], vec["s"][:, :], top[:, 0:1], 0.0, ALU.add, ALU.max)
                    dve.drain()
                    ve.tensor_scalar(vec["keep"][:, :], vec["tmp2"][:, :], 0.0, None, ALU.is_le)
                    dve.drain()
                    ve.tensor_scalar(vec["tmp2"][:, :], vec["tmp2"][:, :], 0.0, None, ALU.min)
                    ve.tensor_scalar(vec["lnc"][:, :], vec["lnc"][:, :], slope - 1.0, None, ALU.mult)
                    if l == 3:
                        ve.tensor_tensor(vec["keep"][:, :], vec["keep"][:, :], vec["valid"][:, :], ALU.mult)
                    dve.drain().then_inc(gaps_ready[l], 1)
                    dve.wait_ge(exps_ready[l], lev + 1)
                    ve.tensor_tensor(vec["v"][:, :], vec["v"][:, :], vec["keep"][:, :], ALU.mult)
                    ve.tensor_tensor(vec["vl"][:, :], vec["vl"][:, :], vec["keep"][:, :], ALU.mult)
                    ve.tensor_scalar(vec["clow"][:, :], vec["clow"][:, :], 1.0 / MASK_F8, None, ALU.mult)
                    dve.drain()
                    ve.tensor_scalar(vec["pow2"][:, :].bitcast(I32), vec["v"][:, :].bitcast(I32), EXP_BITS, None,
                                     ALU.bitwise_and)
                    ve.tensor_scalar(vec["mant"][:, :].bitcast(I32), vec["v"][:, :].bitcast(I32), MANT_BITS, ONE_BITS,
                                     ALU.bitwise_and, ALU.bitwise_or)
                    dve.drain()
                    ve.tensor_scalar(vec["pow2"][:, :], vec["pow2"][:, :], 1.0 / MASK, None, ALU.mult)
                    dve.drain().then_inc(scales_ready[l], 1)

                    if l == 3:
                        first_pass(lev)

                    def parts(c):
                        at = bass.ds(c * GB, GB)
                        for k, scale in enumerate((vec["mant"], vec["vl"])):
                            ve.tensor_tensor(tmp[:, k, :, :], e[:, at, 0:E], over(scale[:, at], E),
                                             ALU.mult).then_inc(prod_ready[l], 1)
                        for k, half in enumerate((xu, xl)):
                            dve.wait_ge(hi_done[l], lev * 2 * NBODY + 2 * c + k + 1)
                            out = ve.tensor_tensor(half[:, at, 1, 0:E], tmp[:, k, :, :], half[:, at, 0, 0:E], ALU.subtract)
                        out.then_inc(parts_ready[l], 1)

                    def cut_masks(g, half, o, opening=False, closing=False):
                        c = half * HO + o
                        if opening:
                            dve.wait_ge(thr_ready[l], 16 * (2 if l == 3 else 1) * (lev * G + g + 1))
                        dve.wait_ge(masks_ready[l][half], 16 * (lev * G + g + 1))
                        first = lev * TILES + g * NB + c * BODY

                        def steps(u0):
                            for u in (u0, u0 + 1):
                                t_of = vec["t"][:, bass.ds(c * BODY + u, 1)]
                                if l != 3 or u % BODY >= N_ACT:
                                    step = ve.tensor_scalar(step8[:, u % 4, :], thr[:, 0, :], t_of, float(MASK),
                                                            ALU.is_le, ALU.mult)
                                if l == 3:
                                    step = ve.tensor_scalar(step8[:, 4 + u % 4, :], thr[:, 1, :], t_of, float(MASK),
                                                            ALU.is_le, ALU.mult)
                                step.then_inc(stepped[l], 1)

                        def lower(u0):
                            dve.wait_ge(upper8[l], first + u0 + 2 + 4)
                            ve.tensor_tensor(two(C8, u0), two(B8, u0), two(C8, u0), ALU.bitwise_xor).then_inc(lower8[l], 2)

                        if opening:
                            steps(0)
                        for u0 in range(0, BODY, 2):
                            n0 = first + u0
                            dve.wait_ge(tile_done[l], n0 + 2)
                            for u in (u0, u0 + 1):
                                pick(words4(C8[:, u, :]), mask_words(half, o), u).then_inc(unpacked[l], 1)
                            if u0 > 0:
                                lower(u0 - 2)
                            dve.wait_ge(stepped[l], n0 + 3)
                            dve.wait_ge(unpacked[l], n0 + 2 + NB)
                            if l == 3:
                                ve.tensor_tensor(two(C8, u0), two(step8, 4 + u0 % 4), two(C8, u0), ALU.bitwise_and) \
                                    .then_inc(kept8, 2)
                                if u0 + 2 < BODY or not closing:
                                    steps(u0 + 2)
                                dve.wait_ge(act_stepped, ((lev * G + g) * NBODY + c) * N_ACT + min(u0 + 2, N_ACT) + 1)
                                dve.wait_ge(kept8, n0 + 2)
                            dve.wait_ge(upper16[l], n0 + 2)
                            ve.tensor_tensor(two(B8, u0), two(step8, u0 % 4), two(C8, u0), ALU.bitwise_and) \
                                .then_inc(upper8[l], 2)
                            if l != 3 and (u0 + 2 < BODY or not closing):
                                steps(u0 + 2)
                        lower(BODY - 2)

                    def finish(g):
                        at = bass.ds(g * GB, GB)
                        dve.wait_ge(bank_read[l], lev * NB + (g + 1) * GB + GB)
                        if l != 3:
                            dve.wait_ge(mean_added, l)
                        ve.tensor_tensor(comb[:, :, 0:E], stage[:, :, E:2 * E], over(vec["clow"][:, at], E), ALU.mult)
                        dve.drain()
                        ve.tensor_tensor(comb[:, :, 0:E], comb[:, :, 0:E], stage[:, :, 0:E], ALU.add)
                        dve.drain().then_inc(stage_used[l], 1)
                        if l != 3:
                            new, f, done = vec["new"][:, at], vec["f"][:, at], vec["done"][:, at]
                            z = comb[:, :, NORM]
                            ve.tensor_scalar(new, z, ROW_SEEN[l] * NORM_SCALE, None, ALU.is_ge)
                            ve.tensor_scalar(f, z, LEAST, None, ALU.max)
                            dve.drain()
                            ve.tensor_tensor(new, new, done, ALU.is_gt)
                            ve.reciprocal(f, f)
                            dve.drain()
                            ve.tensor_tensor(done, done, new, ALU.max)
                            ve.scalar_tensor_tensor(out=f, in0=f, scalar=one["knorm"][:, kw:kw + 1], in1=new,
                                                    op0=ALU.mult, op1=ALU.mult)
                            dve.drain()
                        ve.tensor_tensor(y[:, :, :], comb[:, :, 0:D], over(vec["f"][:, at], D), ALU.mult)
                        dve.drain()
                        if l == 1:
                            ve.tensor_scalar(y[:, :, :], y[:, :, :], 0.0, None, ALU.max)
                            dve.drain()
                        if l == 3:
                            flat = y[:, :, :].rearrange("p b d -> p (b d)")
                            ve.scalar_tensor_tensor(out=y[:, :, :], in0=e[:, at, 0:D], scalar=one["unscale"][:, kw:kw + 1],
                                                    in1=y[:, :, :], op0=ALU.mult, op1=ALU.add)
                            dve.drain()
                            ve.tensor_scalar(comb[:, :, 0:D], y[:, :, :], 0.0, None, ALU.min).then_inc(elu_neg, 1)
                            dve.wait_ge(elu_exp, lev * G + g + 1)
                            ve.scalar_tensor_tensor(out=y[:, :, :], in0=y[:, :, :], scalar=0.0, in1=comb[:, :, 0:D],
                                                    op0=ALU.max, op1=ALU.add)
                            dve.drain()
                            ve.scalar_tensor_tensor(out=y[:, :, :], in0=y[:, :, :], scalar=-1.0,
                                                    in1=over(vec["new"][:, at], D), op0=ALU.add, op1=ALU.mult)
                            dve.drain()
                        ve.tensor_tensor(x[:, at, :], x[:, at, :], y[:, :, :], ALU.add)
                        if l != 3:
                            dve.drain()
                            for k in range(GB):
                                ve.bn_stats(stats8[:, k, :], x[:, bass.ds(g * GB + k, 1), :].rearrange("p a w -> p (a w)"))
                            fold(stats8[:, :, :], vec["mu"][:, at], vec["var"][:, at])

                    parts(0)
                    cut_masks(0, 0, 0, opening=True)
                    with dve.Fori(1, HO) as o:
                        parts(o)
                        cut_masks(0, 0, o)
                    with dve.Fori(0, HO - 1) as o:
                        parts(o + HO)
                        cut_masks(0, 1, o)
                    parts(NBODY - 1)
                    cut_masks(0, 1, HO - 1, closing=True)
                    with dve.Fori(1, G) as g:
                        cut_masks(g, 0, 0, opening=True)
                        finish(g - 1)
                        with dve.Fori(1, HO) as o:
                            cut_masks(g, 0, o)
                        with dve.Fori(0, HO - 1) as o:
                            cut_masks(g, 1, o)
                        cut_masks(g, 1, HO - 1, closing=True)
                    finish(G - 1)
                    dve.drain()
                    ve.tensor_scalar(top[:, :], top[:, :], -WINDOW[l], None, ALU.add)
                    dve.drain()
            dve.drain().then_inc(x_final, 1)


_INS = ["x", "adj", "L1_gnn_W", "L1_gnn_a", "L2_gnn_W", "L2_gnn_a", "L3_gnn_W", "L3_gnn_a"]


def kernel(**inputs):
    import numpy as _np
    import concourse.bacc as _bacc
    from concourse import mybir as _mybir
    from concourse.bass_utils import run_bass_kernel_spmd as _run

    nc = _bacc.Bacc("TRN2", target_bir_lowering=False, num_devices=1)
    arrays, args = {}, []
    for name in _INS:
        a = _np.ascontiguousarray(inputs[name])
        arrays[f"in_{name}_dram"] = a
        args.append(nc.dram_tensor(f"in_{name}_dram", a.shape, _mybir.dt.from_np(a.dtype), kind="ExternalInput").ap())
    out = nc.dram_tensor("out_0_dram", inputs["x"].shape, _mybir.dt.from_np(_np.dtype("float32")), kind="ExternalOutput").ap()
    build_layers(nc, *args, out)
    r = _run(nc, [arrays], core_ids=[0])
    return r.results[0]["out_0_dram"]
```

```python
from contextlib import ExitStack, nullcontext

import concourse.bass as bass
from concourse import mybir
import numpy as np

ALU = mybir.AluOpType
ACT = mybir.ActivationFunctionType
AX_X = mybir.AxisListType.X
F32 = mybir.dt.float32
F16 = mybir.dt.float16
BF16 = mybir.dt.bfloat16
F8 = mybir.dt.float8e4
I32 = mybir.dt.int32
U8 = mybir.dt.uint8
U16 = mybir.dt.uint16

P = 128
D = 128
NORM = D
E = D + 1
EP = E + 1
MASK = 64
MASK_F8 = 2.0
THR = 1e-4
SLOPE = {1: 0.01, 2: 0.2, 3: 0.2}
WINDOW = {1: 70.0, 2: 40.0, 3: 10.0}
ROW_SEEN = {l: float(np.exp(-w - 0.5)) for l, w in WINDOW.items()}
MAX_LEVELS = 1 << 12
H_SCALE = 1024.0
NORM_SCALE = 16384.0
E_BOUND = 1024.0
E_MORE = 2.0
EPS = 1e-5
ROW_SUM_LEAST = 2.0 ** -60
FAR = 2.0 ** 60
LEAST = 1e-30
ADJ_COLS = 2048
UB = 4
EXP_BITS, MANT_BITS, ONE_BITS = 0x7F800000, 0x007FFFFF, 0x3F800000
RING = 8
B16_RING = 4


def build_layers(nc, x_in, adj_in, w1, a1, w2, a2, w3, a3, x_out):
    N = x_in.shape[0]
    NB = N // P
    GB = 8
    G = NB // GB
    GW = GB * P
    CJ = 4
    BODY = 8
    NBODY = NB // BODY
    TILES = G * NB
    NCOL = N // ADJ_COLS
    LAYERS = (1, 2, 3)
    WIDTH = {1: E, 2: E, 3: D}
    N_ACT = 3
    Z_ACT = 5
    Z_DVE = BODY - Z_ACT

    OCT = NB // 8
    HO = OCT // 2
    QG = GB // 2
    LEAD = 3
    PLANES = 8 // NCOL

    mask_dram = nc.dram_tensor("mask_dram", [NB // 2, P, OCT, 2 * P], U8, kind="Internal").ap()
    row_dram = [nc.dram_tensor(f"row_dram{l}", [3, NB, P], F32, kind="Internal").ap() for l in range(4)]

    with ExitStack() as ctx:
        def sb(name, shape, dt):
            return ctx.enter_context(nc.sbuf_tensor(name, shape, dt))

        def sem(name):
            return ctx.enter_context(nc.semaphore(name))

        def per_layer(name, layers=LAYERS):
            return {l: sem(f"{name}{l}") for l in layers}

        x = sb("x", [P, NB, D], F32)
        e = sb("e", [P, NB, EP], F32)
        xu = sb("xu", [P, NB, 2, EP], F16)
        xl = sb("xl", [P, NB, 2, EP], F16)
        xl_now = sb("xl_now", [P, 2, CJ, 2, EP], F16)
        ring = sb("ring", [P, 24 * 1024], U8)
        work = sb("work", [P, GB * 258], F32)
        comb = sb("comb", [P, GB, EP], F32)
        y = sb("y", [P, GB, D], F32)
        thr = sb("thr", [P, 2, GW], F32)
        masks = sb("masks", [P, 2, QG, HO, 2 * P], U8)
        step8 = sb("step8", [P, 8, GW], U8)
        ident = sb("ident", [P, P], F32)
        w_ea = sb("w_ea", [P, 3, EP], F32)
        a_col = sb("a_col", [P, 3, 2], F32)
        vec = {n: sb(f"v_{n}", [P, NB], F32) for n in (
            "mu", "rstd", "tmp", "tmp2", "s", "t", "keep", "v", "vl", "pow2", "mant", "clow",
            "lnc", "empty", "done", "new", "f", "z", "rest", "valid")}
        one = {n: sb(f"c_{n}", [P, 3], F32) for n in ("n2", "p2", "scale", "unscale", "knorm")}
        tm = sb("tm", [P, 2], F32)
        tmr = sb("tmr", [P, 2], F32)
        top = sb("top", [P, 1], F32)
        levels_f = sb("levels_f", [P, 1], F32)
        levels = sb("levels", [P, 3], I32)
        rows = sb("rows", [NB, 2, P], F32)
        vz = sb("vz", [P, NB, 10], BF16)
        stats8 = sb("stats8", [P, GB, 6], F32)
        vz_now = sb("vz_now", [P, 2, CJ, 10], BF16)
        psum = ctx.enter_context(nc.psum_tensor("psum", [P, 8, 512], F32))

        w_e, w_a = w_ea[:, :, 0:D], w_ea[:, :, D:EP]
        ones = y[:, 0, :]
        w_raw = comb[:, :, :].rearrange("p b w -> p (b w)")[:, 0:3 * D].rearrange("p (k d) -> p k d", k=3)
        tmp = work[:, 0:2 * GB * E].rearrange("p (s b w) -> p s b w", s=2, b=GB)
        stage = work[:, :].rearrange("p (b w) -> p b w", b=GB)
        zs = work[:, 0:NB * 10].rearrange("p (b w) -> p b w", b=NB)
        zr = work[:, NB * 10:NB * 13].rearrange("p (b w) -> p b w", b=NB)
        mean = vz[:, :, :].rearrange("p b w -> p (b w)").bitcast(F32)[:, 0:D]
        vec["var"] = vec["z"]
        vec["t_far"] = vec["empty"]
        stats = work[:, 0:NB * 6].rearrange("p (b w) -> p b w", b=NB)
        w_t = work[:, 1024:1024 + 3 * D].rearrange("p (k d) -> p k d", k=3)
        B8 = ring[:, 0:8192].rearrange("p (s w) -> p s w", s=RING)
        C8 = ring[:, 8192:16384].rearrange("p (s w) -> p s w", s=RING)
        B16 = ring[:, 16384:24576].bitcast(BF16).rearrange("p (s w) -> p s w", s=B16_RING)
        xu_now = ring[:, 16384:16384 + 2 * CJ * 2 * EP * 2].bitcast(F16).rearrange(
            "p (s c h w) -> p s c h w", s=2, c=CJ, h=2)
        z_step = ring[:, 16384:24576].rearrange("p (s w) -> p s w", s=RING)
        planes8 = ring[:, 0:2 * N].rearrange("p (s k o w) -> p s k o w", s=2, k=8, o=OCT)
        packed8 = masks[:, :, :, :, :].rearrange("p s q o w -> p (s q o w)")[:, 0:2 * OCT * 2 * P].rearrange(
            "p (s o w) -> p s o w", s=2, o=OCT)
        bits = thr[:, :, :].rearrange("p s w -> p (s w)").bitcast(BF16)[:, 0:8 * P].rearrange("p (k w) -> p k w", k=8)
        hT = ring[:, 0:4096].bitcast(F32).rearrange("p (s w) -> p s w", s=2)
        hs = ring[:, 16384:20480].bitcast(F32).rearrange("p (s w) -> p s w", s=2)
        hr = ring[:, 20480:24576].bitcast(F32).rearrange("p (s w) -> p s w", s=2)
        adj_sb = e[:, :, :].rearrange("p b w -> p (b w)")[:, 0:NCOL * ADJ_COLS].bitcast(I32).rearrange("p (c w) -> p c w", c=NCOL)
        adj_bf = xl[:, :, :, :].rearrange("p a b c -> p (a b c)")[:, 0:NCOL * ADJ_COLS].bitcast(BF16).rearrange("p (c w) -> p c w", c=NCOL)

        def words4(ap):
            return ap.bitcast(U16).rearrange("p (q w) -> p q w", q=QG)

        def mask_words(half, o):
            return masks[:, half, :, bass.ds(o, 1), :].rearrange("p q a i -> p q (a i)").bitcast(U16)

        def two(tiles, slot):
            return tiles[:, slot:slot + 2, :].rearrange("p s w -> p (s w)").bitcast(U16)

        def splits_of(g):
            return thr[:, bass.ds(g & 1, 1), :].rearrange("p a w -> p (a w)")

        def pick(out, packed, k):
            both = (MASK << 8) | MASK
            if k <= 6:
                return nc.vector.tensor_scalar(out, packed, 6 - k, both, ALU.logical_shift_left, ALU.bitwise_and)
            return nc.vector.tensor_scalar(out, packed, 1, both, ALU.logical_shift_right, ALU.bitwise_and)

        def over(v, width):
            return v.unsqueeze(2).to_broadcast([P, v.shape[1], width])

        x_loaded, w_loaded, const_ready = sem("x_loaded"), sem("w_loaded"), sem("const_ready")
        w_trans, w_copied, w_proj, norm2_ready, w_norm, w_ready = (sem(n) for n in (
            "w_trans", "w_copied", "w_proj", "norm2_ready", "w_norm", "w_ready"))
        adj_loaded = [sem(f"adj_loaded{c}") for c in range(NCOL)]
        adj_masked, packed = sem("adj_masked"), sem("packed")
        evacuated = sem("evacuated")
        planes = sem("planes")
        sums_done = sem("sums_done")
        sums_read = sem("sums_read")
        mask_stored = [sem(f"mask_stored{s}") for s in range(2)]
        h_used = sem("h_used")
        ALL = (0,) + LAYERS
        var_ready, std_ready = sem("var_ready"), sem("std_ready")
        h_raw, h_ready = (per_layer(n, ALL) for n in ("h_raw", "h_ready"))
        hi_ready = sem("hi_ready")
        h_trans, hT_ready, e_made, e_ready = (per_layer(n) for n in ("h_trans", "hT_ready", "e_made", "e_ready"))
        t_range, t_range_all, levels_ready = (sem(n) for n in ("t_range", "t_range_all", "levels_ready"))
        neg_s, neg_s_trans, neg_s_row, neg_s_stored = (sem(n) for n in ("neg_s", "neg_s_trans", "neg_s_row", "neg_s_stored"))
        gaps_ready, exps_ready, scales_ready = (per_layer(n) for n in ("gaps_ready", "exps_ready", "scales_ready"))
        prod_ready, hi_done, parts_ready = (per_layer(n) for n in ("prod_ready", "hi_done", "parts_ready"))
        pe_gated, sp_gated, act_gated = sem("pe_gated"), sem("sp_gated"), sem("act_gated")
        thr_ready = per_layer("thr_ready")
        masks_ready = {l: [sem(f"masks_ready{l}_{s}") for s in range(2)] for l in LAYERS}
        unpacked = per_layer("unpacked")
        stepped, kept8 = per_layer("stepped"), sem("kept8")
        act_stepped = sem("act_stepped")
        upper8 = per_layer("upper8")
        lower8 = per_layer("lower8")
        upper16 = per_layer("upper16")
        xl_loaded = {l: [sem(f"xl_loaded{l}_{s}") for s in range(2)] for l in LAYERS}
        tile_done = per_layer("tile_done")
        bank_done = per_layer("bank_done")
        bank_read = per_layer("bank_read")
        stage_used = per_layer("stage_used")
        mean_added = sem("mean_added")
        z_parts, z_thr_ready, z_stepped, z_upper8, z_read = (sem(n) for n in (
            "z_parts", "z_thr_ready", "z_stepped", "z_upper8", "z_read"))
        z_columns, z_act_stepped = sem("z_columns"), sem("z_act_stepped")
        z_unpacked = sem("z_unpacked")
        z_tile = sem("z_tile")
        z_masks_ready = [sem(f"z_masks_ready{s}") for s in range(2)]
        row_sum, row_ln, cuts, cuts_trans, cut_rows, cut_stored = (sem(n) for n in (
            "row_sum", "row_ln", "cuts", "cuts_trans", "cut_rows", "cut_stored"))
        elu_neg, elu_exp, elu_pos = sem("elu_neg"), sem("elu_exp"), sem("elu_pos")
        elu_added = sem("elu_added")
        x_final, x_stored = sem("x_final"), sem("x_stored")

        def n_levels(eng, l):
            eng.wait_ge(levels_ready, l)
            return eng.value_load(levels[0:1, l - 1:l], min_val=1, max_val=MAX_LEVELS)

        block = ctx.enter_context(nc.Block())

        @block.sync
        def _(sp):
            def gate():
                sp.nop().then_inc(sp_gated, 1)

            sp.dma_start(x[:, :, :], x_in.rearrange("(b p) d -> p b d", p=P)).then_inc(x_loaded, 16)
            for k, (w, a) in enumerate(((w1, a1), (w2, a2), (w3, a3))):
                sp.dma_start(w_raw[:, k, :], w).then_inc(w_loaded, 16)
                with nc.allow_non_contiguous_dma(reason="256 numbers"):
                    sp.dma_start(a_col[:, k, :], a.rearrange("(h p) o -> p (h o)", p=P)).then_inc(w_loaded, 16)

            adj_rows = adj_in.rearrange("(b p) (c w) -> c b p w", p=P, w=ADJ_COLS)
            for first in (True, False):
                with nullcontext(0) if first else sp.Fori(1, NB) as b:
                    for c in range(NCOL):
                        if not first:
                            sp.wait_ge(adj_masked, (b - 1) * NCOL + c + 1)
                        sp.dma_start(adj_sb[:, c, :], adj_rows[c, bass.ds(b, 1)].rearrange("a p w -> (a p) w")) \
                            .then_inc(adj_loaded[c], 16)

            def load_masks(ready, g, half):
                sp.dma_start(masks[:, half].rearrange("p q o i -> p q (o i)"),
                             mask_dram[bass.ds(g * QG, QG), :, half * HO:(half + 1) * HO, :].rearrange(
                                 "q p o i -> p q (o i)")).then_inc(ready[half], 16)

            def load_thr(l, which, row, g, ready):
                slot = bass.ds(which, 1)
                sp.dma_start(thr[:, slot, :].rearrange("p a w -> p (a w)"),
                             row_dram[l][row, bass.ds(g * GB, GB), :].rearrange("b p -> (b p)")
                             .partition_broadcast(P)).then_inc(ready, 16)

            for l in LAYERS:
                sp.wait_ge(neg_s_row, l)
                sp.dma_start(row_dram[l][0, :, :], rows[:, 0, :]).then_inc(neg_s_stored, 16)
                sp.wait_ge(neg_s_stored, 16 * l)
                if l == 1:
                    for s in range(2):
                        sp.wait_ge(mask_stored[s], 16 * (NB // 4) + 16)
                n_lev = n_levels(sp, l)
                with sp.Fori(0, n_lev) as lev:
                    if l == 3:
                        sp.wait_ge(lower8[3], lev * TILES + 1)
                        gate()
                        with sp.Fori(0, G) as g:
                            for half in range(2):
                                sp.wait_ge(z_unpacked, lev * TILES + g * NB + (half + 1) * (NB // 2))
                                gate()
                                load_masks(z_masks_ready, g, half)
                                if half == 0:
                                    sp.wait_ge(z_stepped, (lev * G + g) * NBODY * Z_DVE + 1)
                                    sp.wait_ge(z_act_stepped, (lev * G + g) * NBODY * Z_ACT + 1)
                                    gate()
                                    load_thr(3, g & 1, 0, g, z_thr_ready)
                        sp.wait_ge(cut_rows, lev + 1)
                        gate()
                        sp.dma_start(row_dram[3][1:3, :, :].rearrange("r b p -> b r p"), rows[:, :, :]) \
                            .then_inc(cut_stored, 16)
                        sp.wait_ge(cut_stored, lev * 16 + 32)
                        gate()
                    with sp.Fori(0, G) as g:
                        for half in range(2):
                            sp.wait_ge(unpacked[l], lev * TILES + g * NB + (half + 1) * (NB // 2))
                            gate()
                            load_masks(masks_ready[l], g, half)
                            if half == 0:
                                sp.wait_ge(stepped[l], lev * TILES + g * NB + 1 + (NB if l == 3 else 0))
                                if l == 3:
                                    sp.wait_ge(act_stepped, (lev * G + g) * (NB // 2) * N_ACT + 1)
                                gate()
                                if l == 3:
                                    load_thr(3, 0, 1, g, thr_ready[3])
                                    load_thr(3, 1, 2, g, thr_ready[3])
                                else:
                                    load_thr(l, g & 1, 0, g, thr_ready[l])
            sp.wait_ge(x_final, 1)
            sp.dma_start(x_out.rearrange("(b p) d -> p b d", p=P), x[:, :, :]).then_inc(x_stored, 16)
            sp.wait_ge(x_stored, 16)

        @block.gpsimd
        def _(pool):
            for s, n in ([(evacuated, 2), (planes, 32), (sums_done, 2), (sums_read, 2), (z_tile, RING),
                          (z_stepped, NBODY * Z_DVE + 1), (z_act_stepped, NBODY * Z_ACT + 1), (act_stepped, 1), (elu_added, 1), (z_upper8, RING), (z_unpacked, NB), (z_read, 1),
                          (mask_stored[0], 16), (mask_stored[1], 16), (cut_stored, 16)]
                         + [(s, n) for l in LAYERS for s, n in (
                             (lower8[l], 1), (unpacked[l], NB), (upper8[l], 4), (upper16[l], RING), (tile_done[l], RING),
                             (bank_read[l], GB), (stage_used[l], 1), (stepped[l], NB + 1))]):
                pool.nop().then_inc(s, n)
            nc.gpsimd.memset(ones[:, :], 1.0)
            nc.gpsimd.memset(ident[:, :], 0.0)
            pool.drain()
            nc.gpsimd.affine_select(out=ident[:, :], in_=ident[:, :], compare_op=ALU.not_equal, fill=1.0, base=0,
                                    pattern=[[-1, P]], channel_multiplier=1)
            pool.drain()
            for k in range(8):
                nc.gpsimd.tensor_scalar(bits[:, k, :], ident[:, :], float(1 << k), None, ALU.mult)
            nc.gpsimd.memset(xu[:, :, 0, NORM:NORM + 1], 1.0)
            nc.gpsimd.memset(xu[:, :, 1, NORM:NORM + 1], 0.0)
            nc.gpsimd.memset(xu[:, :, :, E:EP], 0.0)
            nc.gpsimd.memset(xl[:, :, :, E:EP], 0.0)
            pool.drain().then_inc(const_ready, 1)

            for l in (1, 2):
                one_pass = lambda b: e[:, b * GB:(b + 1) * GB, 0:D]
                pool.wait_ge(t_range, l)
                nc.gpsimd.partition_all_reduce(tmr[:, :], tm[:, :], P, bass.bass_isa.ReduceOp.max) \
                    .then_inc(t_range_all, 1)
                pool.wait_ge(e_ready[l], NB // UB)
                nc.gpsimd.tensor_tensor(y[:, :, :], one_pass(0), one_pass(1), ALU.add)
                for b in range(2, NB // GB):
                    pool.drain()
                    nc.gpsimd.tensor_tensor(y[:, :, :], y[:, :, :], one_pass(b), ALU.add)
                half = GB // 2
                while half:
                    pool.drain()
                    nc.gpsimd.tensor_tensor(y[:, 0:half, :], y[:, 0:half, :], y[:, half:2 * half, :], ALU.add)
                    half //= 2
                pool.drain()
                nc.gpsimd.partition_all_reduce(mean[:, :], y[:, 0, :], P, bass.bass_isa.ReduceOp.add)
                pool.drain()
                nc.gpsimd.tensor_scalar(mean[:, :], mean[:, :], one["unscale"][:, l - 1:l], 1.0 / N, ALU.mult, ALU.mult)
                if l == 1:
                    pool.drain()
                    nc.gpsimd.tensor_scalar(mean[:, :], mean[:, :], 0.0, None, ALU.max)
                with pool.Fori(0, G) as g:
                    pool.drain()
                    nc.gpsimd.tensor_tensor(y[:, :, :], mean[:, :].unsqueeze(1).to_broadcast([P, GB, D]),
                                            over(vec["empty"][:, bass.ds(g * GB, GB)], D), ALU.mult)
                    pool.drain()
                    nc.gpsimd.tensor_tensor(x[:, bass.ds(g * GB, GB), :], x[:, bass.ds(g * GB, GB), :], y[:, :, :], ALU.add)
                pool.drain().then_inc(mean_added, 1)
            pool.wait_ge(t_range, 3)
            nc.gpsimd.partition_all_reduce(tmr[:, :], tm[:, :], P, bass.bass_isa.ReduceOp.max) \
                .then_inc(t_range_all, 1)
            n_lev = n_levels(pool, 3)
            with pool.Fori(0, n_lev) as lev:
                with pool.Fori(0, G) as g:
                    at = bass.ds(g * GB, GB)
                    pool.wait_ge(elu_pos, lev * G + g + 1)
                    pool.wait_ge(elu_exp, lev * G + g + 1)
                    nc.gpsimd.tensor_tensor(y[:, :, :], y[:, :, :], comb[:, :, 0:D], ALU.add)
                    pool.drain()
                    nc.gpsimd.tensor_tensor(y[:, :, :], y[:, :, :], over(vec["new"][:, at], D), ALU.mult)
                    pool.drain()
                    nc.gpsimd.tensor_tensor(x[:, at, :], x[:, at, :], y[:, :, :], ALU.add)
                    pool.drain().then_inc(elu_added, 1)

        @block.tensor
        def _(pe):
            def gate():
                pe.nop().then_inc(pe_gated, 1)

            pe.wait_ge(w_loaded, 16 * 6)
            pe.wait_ge(const_ready, 1)
            for k in range(3):
                mm = nc.tensor.transpose(psum[:, 5, k * P:(k + 1) * P], w_raw[:, k, :], ident[:, :])
            mm.then_inc(w_trans, 1)
            pe.wait_ge(w_copied, 1)
            for k in range(3):
                w_out_in = w_raw[:, k, :] if k == 0 else w_t[:, k, :]
                mm = nc.tensor.matmul(psum[:, 6, 2 * k:2 * k + 2], w_out_in, a_col[:, k, :], start=True, stop=True)
                mm = nc.tensor.matmul(psum[:, 7, k * P:(k + 1) * P], ones[:, :], w_e[:, k, :], start=True, stop=True)
            mm.then_inc(w_proj, 1)

            def pack(b, slot, c):
                pe.wait_ge(adj_masked, b * NCOL + c + 1)
                if c == 0:
                    pe.wait_ge(evacuated, b + 1)
                for o in (2 * c, 2 * c + 1):
                    for k in range(8):
                        at = (8 * (o % 2) + k) * P
                        mm = nc.tensor.matmul(psum[:, 2 * slot + o // 4, o % 4 * P:(o % 4 + 1) * P],
                                              adj_bf[:, c, at:at + P], bits[:, k, :],
                                              start=(o % 4 == 0 and k == 0), stop=True, skip_group_check=True)
                mm.then_inc(packed, 1)

            def sums(b, slot, c):
                if c == 0:
                    pe.wait_ge(sums_read, b + 1)
                pe.wait_ge(planes, 8 * b + (c + 1) * PLANES + 32)
                gate()
                for k in range(c * PLANES, (c + 1) * PLANES):
                    for o in range(OCT):
                        for part in range(2):
                            mm = nc.tensor.matmul(psum[:, 4 + slot, 0:E], planes8[:, slot, k, o, :].bitcast(F8),
                                                  xu[:, 8 * o + k, part, 0:E], start=(k == 0 and o == 0 and part == 0),
                                                  stop=(k == 7 and o == OCT - 1 and part == 1), skip_group_check=True)
                if c == NCOL - 1:
                    mm.then_inc(sums_done, 1)

            pe.wait_ge(w_norm, 1)
            for b in range(LEAD):
                for c in range(NCOL):
                    pack(b, b % 2, c)
            pe.wait_ge(h_used, NB // UB)
            with pe.Fori(0, (NB - 4) // 2) as i:
                for u in range(2):
                    for c in range(NCOL):
                        pack(2 * i + u + LEAD, (u + LEAD) % 2, c)
                        sums(2 * i + u, u, c)
            for b in range(NB - 4, NB):
                for c in range(NCOL):
                    if b + LEAD < NB:
                        pack(b + LEAD, (b + LEAD) % 2, c)
                    sums(b, b % 2, c)

            for l in LAYERS:
                k_w = l - 1
                if l == 1:
                    pe.wait_ge(w_ready, 1)

                def transpose_h(unit, s, first):
                    pe.wait_ge(h_ready[l], unit + 1)
                    if not first:
                        pe.wait_ge(hT_ready[l], unit - 1)
                    for k in range(UB):
                        mm = nc.tensor.transpose(psum[:, s, k * P:(k + 1) * P], hr[:, s, k * P:(k + 1) * P], ident[:, :])
                    mm.then_inc(h_trans[l], 1)

                def project(unit, s, first):
                    pe.wait_ge(hT_ready[l], unit + 1)
                    if not first:
                        pe.wait_ge(e_ready[l], unit - 1)
                    for k in range(UB):
                        mm = nc.tensor.matmul(psum[:, 2 + 2 * s + k // 2, k % 2 * EP:(k % 2 + 1) * EP],
                                              hT[:, s, k * P:(k + 1) * P], w_ea[:, k_w, :], start=True, stop=True)
                    mm.then_inc(e_made[l], 1)

                NU = NB // UB
                for u in range(2):
                    transpose_h(u, u, True)
                for u in range(2):
                    project(u, u, True)
                    transpose_h(u + 2, u, False)
                with pe.Fori(1, NU // 2 - 1) as i:
                    for u in range(2):
                        project(2 * i + u, u, False)
                        transpose_h(2 * i + u + 2, u, False)
                for u in range(2):
                    project(NU - 2 + u, u, False)
                pe.wait_ge(neg_s, l)
                nc.tensor.transpose(psum[0:NB, 5, 0:P], vec["tmp"][:, :], ident[:, :]).then_inc(neg_s_trans, 1)

                n_lev = n_levels(pe, l)
                with pe.Fori(0, n_lev) as lev:
                    if l == 3:
                        pe.wait_ge(z_parts, lev + 1)
                        gate()
                        with pe.Fori(0, G) as g:
                            pe.wait_ge(z_read, lev * G + g + 1)
                            for first in (True, False):
                                with nullcontext(0) if first else pe.Fori(1, NBODY) as c:
                                    for u in range(BODY):
                                        n = lev * TILES + g * NB + c * BODY + u
                                        pe.wait_ge(z_upper8, n + 1 + RING)
                                        if u % CJ == 0:
                                            pe.wait_ge(z_columns, lev * (TILES // CJ) + g * (NB // CJ) + c * 2 + u // CJ + 1)
                                        gate()
                                        for b in range(GB):
                                            nc.tensor.matmul(psum[:, b, 0:6], B8[:, u, b * P:(b + 1) * P].bitcast(F8),
                                                             vz_now[:, u // CJ, u % CJ, 0:6],
                                                             start=(first and u == 0), stop=True, skip_group_check=True)
                                            mm = nc.tensor.matmul(psum[:, b, 6:10],
                                                                  C8[:, u, b * P:(b + 1) * P].bitcast(F8),
                                                                  vz_now[:, u // CJ, u % CJ, 6:10],
                                                                  start=False, stop=True, skip_group_check=True)
                                        mm.then_inc(z_tile, 1)
                        pe.wait_ge(cuts, lev + 1)
                        gate()
                        nc.tensor.transpose(psum[0:NB, 0, 0:P], vec["tmp"][:, :], ident[:, :])
                        nc.tensor.transpose(psum[0:NB, 0, P:2 * P], vec["tmp2"][:, :], ident[:, :]).then_inc(cuts_trans, 1)
                        pe.wait_ge(cut_rows, lev + 1)
                        gate()
                    with pe.Fori(0, G) as g:
                        for first in (True, False):
                            with nullcontext(0) if first else pe.Fori(1, NBODY) as c:
                                pe.wait_ge(parts_ready[l], lev * NBODY + c + 1)
                                for u in range(BODY):
                                    n, W = lev * TILES + g * NB + c * BODY + u, WIDTH[l]
                                    pe.wait_ge(lower8[l], n + 2)
                                    if u % CJ == 0:
                                        pe.wait_ge(xl_loaded[l][u // CJ],
                                                   (32 if l == 3 else 16) * (lev * G * NBODY + g * NBODY + c + 1))
                                    if l == 3:
                                        gate()
                                    else:
                                        pe.wait_ge(upper16[l], n + 1 + RING)
                                    for b in range(GB):
                                        if first and u == 0:
                                            pe.wait_ge(bank_read[l], lev * NB + g * GB + b + 1)
                                            if l == 3:
                                                gate()
                                        rows_b = slice(b * P, (b + 1) * P)
                                        for part in range(2):
                                            if l == 3:
                                                weights, x_part = B8[:, u, rows_b].bitcast(F8), xu_now[:, u // CJ, u % CJ, part, 0:W]
                                            else:
                                                weights = B16[:, u % B16_RING, rows_b]
                                                x_part = xu[:, bass.ds(c * BODY + u, 1), part, 0:W].rearrange("p a w -> p (a w)")
                                            mm = nc.tensor.matmul(psum[:, b, 0:W], weights, x_part,
                                                                  start=(first and u == 0 and part == 0), stop=True,
                                                                  skip_group_check=True)
                                        for part in range(2):
                                            mm = nc.tensor.matmul(psum[:, b, W:2 * W], C8[:, u, rows_b].bitcast(F8),
                                                                  xl_now[:, u // CJ, u % CJ, part, 0:W],
                                                                  start=False, stop=True, skip_group_check=True)
                                        if u == BODY - 1 and b < GB - 1:
                                            mm.then_inc(bank_done[l], 1)
                                    mm.then_inc(tile_done[l], 1)

        @block.scalar
        def _(act):
            act.wait_ge(norm2_ready, 1)
            nc.scalar.activation(one["n2"][:, :], one["n2"][:, :], ACT.Sqrt).then_inc(w_norm, 1)

            def normalise(l):
                act.wait_ge(var_ready, l + 1)
                nc.scalar.activation(vec["rstd"][:, :], vec["var"][:, :], ACT.Sqrt).then_inc(std_ready, 1)

            def relu(l, unit, s, first):
                act.wait_ge(h_raw[l], unit + 1)
                if not first:
                    act.wait_ge(h_used if l == 0 else h_trans[l], unit - 1)
                nc.scalar.activation(hr[:, s, :], hs[:, s, :], ACT.Relu).then_inc(h_ready[l], 1)

            def blocks(s):
                return hr[:, s, :].rearrange("p (b d) -> p b d", b=UB)

            def evacuate(b, u):
                slot = u // 2
                act.wait_ge(packed, (b + 1) * NCOL)
                act.wait_ge(planes, 8 * b + 8)
                nc.scalar.activation(packed8[:, slot, :, u % 2 * P:(u % 2 + 1) * P],
                                     psum[:, 2 * (u % 2):2 * (u % 2) + 2, :].rearrange("p k (o w) -> p (k o) w", w=P)
                                     [:, 0:OCT, :], ACT.Copy).then_inc(evacuated, 1)

            def store(pair, slot, b):
                act.wait_ge(evacuated, b + 1 + 2)
                act.dma_start(mask_dram[bass.ds(pair, 1)].rearrange("a p o i -> p (a o) i"), packed8[:, slot]) \
                    .then_inc(mask_stored[slot], 16)

            def stored_before(slot, count):
                act.wait_ge(mask_stored[slot], 16 * count + 16)

            normalise(0)
            QUARTER = NB // UB // 4 // 2
            for quarter in range(4):
                for first in (True, False) if quarter == 0 else (False,):
                    begin, end = quarter * QUARTER + (quarter == 0), (quarter + 1) * QUARTER
                    if not first and begin == end:
                        continue
                    with nullcontext(0) if first else act.Fori(begin, end) as i:
                        for s in range(2):
                            unit = 2 * i + s
                            relu(0, unit, s, first)
                            act.wait_ge(h_ready[0], unit + 1)
                            nc.scalar.activation(xu[:, bass.ds(unit * UB, UB), 0, 0:D], blocks(s), ACT.Copy,
                                                 scale=H_SCALE).then_inc(hi_ready, 1)
                if quarter < LEAD:
                    evacuate(quarter, quarter)
                    if quarter == 1:
                        store(0, 0, 1)

            with act.Fori(0, (NB - 4) // 4) as i:
                evacuate(4 * i + 3, 3)
                store(2 * i + 1, 1, 4 * i + 3)
                stored_before(0, i + 1)
                evacuate(4 * i + 4, 0)
                evacuate(4 * i + 5, 1)
                store(2 * i + 2, 0, 4 * i + 5)
                stored_before(1, i + 1)
                evacuate(4 * i + 6, 2)
            evacuate(NB - 1, 3)
            store(NB // 2 - 1, 1, NB - 1)

            for l in LAYERS:
                slope = SLOPE[l]
                normalise(l)

                def e_out(unit, s):
                    act.wait_ge(e_made[l], unit + 1)
                    nc.scalar.activation(e[:, bass.ds(unit * UB, UB), :].rearrange("p (k b) w -> p k (b w)", k=2),
                                         psum[:, 2 + 2 * s:4 + 2 * s, 0:2 * EP], ACT.Copy) \
                        .then_inc(e_ready[l], 1)

                NU = NB // UB
                for u in range(2):
                    relu(l, u, u, True)
                with act.Fori(0, NU // 2 - 1) as i:
                    for u in range(2):
                        relu(l, 2 * i + u + 2, u, False)
                        e_out(2 * i + u, u)
                for u in range(2):
                    e_out(NU - 2 + u, u)

                n_lev = n_levels(act, l)
                with act.Fori(0, n_lev) as lev:
                    act.wait_ge(gaps_ready[l], lev + 1)
                    nc.scalar.activation(vec["v"][:, :], vec["tmp2"][:, :], ACT.Exp)
                    nc.scalar.activation(vec["vl"][:, :], vec["tmp2"][:, :], ACT.Exp, scale=slope)
                    nc.scalar.activation(vec["clow"][:, :], vec["lnc"][:, :], ACT.Exp).then_inc(exps_ready[l], 1)

                    if l == 3:
                        def z_columns_of(g, c, k):
                            act.wait_ge(z_tile, lev * TILES + g * NB + c * BODY + (k + 1) * CJ)
                            nc.scalar.activation(vz_now[:, k, :, :], vz[:, bass.ds(c * BODY + k * CJ, CJ), :],
                                                 ACT.Copy).then_inc(z_columns, 1)

                        def z_steps(g, c, tiles):
                            for u in tiles:
                                act.wait_ge(z_upper8, lev * TILES + g * NB + c * BODY + u + 1)
                                if isinstance(c, int):
                                    act.nop().then_inc(act_gated, 1)
                                nc.scalar.activation(z_step[:, u % RING, :], splits_of(g), ACT.Relu,
                                                     bias=vec["t_far"][:, bass.ds(c * BODY + u, 1)], scale=-FAR) \
                                    .then_inc(z_act_stepped, 1)

                        act.wait_ge(z_parts, lev + 1)
                        def z_body(g, c, closing=False):
                            z_columns_of(g, c, 0)
                            z_steps(g, c, range(2, 4))
                            z_columns_of(g, c, 1)
                            z_steps(g, c, range(4, Z_ACT))
                            if not closing:
                                z_steps(g, c, range(BODY, BODY + 2))

                        def z_group(g, last):
                            with act.Fori(0, NBODY - 1) as c:
                                z_body(g, c)
                            z_body(g, NBODY - 1, closing=True)
                            if not last:
                                act.wait_ge(z_thr_ready, 16 * (lev * G + g + 2))
                                z_steps(g + 1, 0, range(0, 2))
                            act.wait_ge(z_tile, lev * TILES + (g + 1) * NB + RING)
                            nc.scalar.activation(zs[:, bass.ds(g * GB, GB), :], psum[:, :, 0:10], ACT.Copy).then_inc(z_read, 1)

                        act.wait_ge(z_thr_ready, 16 * (lev * G + 1))
                        z_steps(0, 0, range(0, 2))
                        with act.Fori(0, G - 1) as g:
                            z_group(g, last=False)
                        z_group(G - 1, last=True)
                        act.wait_ge(row_sum, lev + 1)
                        nc.scalar.activation(vec["z"][:, :], vec["z"][:, :], ACT.Ln).then_inc(row_ln, 1)

                    def hi(c):
                        for k, half in enumerate((xu, xl)):
                            act.wait_ge(prod_ready[l], lev * 2 * NBODY + 2 * c + k + 1)
                            nc.scalar.activation(half[:, bass.ds(c * GB, GB), 0, 0:E], tmp[:, k, :, :], ACT.Copy) \
                                .then_inc(hi_done[l], 1)

                    def next_parts(g, c, u):
                        act.wait_ge(tile_done[l], lev * TILES + g * NB + c * BODY + u - CJ + RING)
                        for now, whole in ((xl_now, xl), (xu_now, xu))[:2 if l == 3 else 1]:
                            act.dma_start(now[:, u // CJ], whole[:, bass.ds(c * BODY + u, CJ)]) \
                                .then_inc(xl_loaded[l][u // CJ], 16)

                    def steps(g, c, pairs):
                        for u in pairs:
                            act.wait_ge(upper8[3], lev * TILES + g * NB + c * BODY + u + 2)
                            for slot, which, tile in ((4 + u % 4, 1, u), (u % 4, 0, u), ((u + 1) % 4, 0, u + 1)):
                                nc.scalar.activation(step8[:, slot, :], thr[:, which, :], ACT.Relu,
                                                     bias=vec["t_far"][:, bass.ds(c * BODY + tile, 1)], scale=-FAR) \
                                    .then_inc(act_stepped, 1)

                    def rest_of_body(g, c, closing=False):
                        steps(g, c, (4, 6))
                        next_parts(g, c, CJ)
                        if not closing:
                            steps(g, c, (8, 10))

                    def scale_upper(g, c, tiles):
                        for u in tiles:
                            n = lev * TILES + g * NB + c * BODY + u
                            if u % CJ == 0:
                                next_parts(g, c, u)
                            act.wait_ge(upper8[l], n + 1 + 4)
                            act.wait_ge(tile_done[l], n + 1 + RING - B16_RING)
                            nc.scalar.activation(B16[:, u % B16_RING, :], B8[:, u, :], ACT.Copy,
                                                 scale=vec["pow2"][:, bass.ds(c * BODY + u, 1)]).then_inc(upper16[l], 1)

                    def read_banks(g):
                        act.wait_ge(stage_used[l], lev * G + g + 1)
                        for b in range(GB):
                            if b < GB - 1:
                                act.wait_ge(bank_done[l], (GB - 1) * (lev * G * NBODY + (g + 1) * NBODY - 1) + b + 1)
                            else:
                                act.wait_ge(tile_done[l], lev * TILES + (g + 1) * NB + RING)
                            nc.scalar.activation(stage[:, b, 0:2 * WIDTH[l]], psum[:, b, 0:2 * WIDTH[l]], ACT.Copy).then_inc(bank_read[l], 1)

                    def elu(g):
                        act.wait_ge(elu_neg, lev * G + g + 1)
                        nc.scalar.activation(comb[:, :, 0:D], comb[:, :, 0:D], ACT.Exp).then_inc(elu_exp, 1)

                    act.wait_ge(scales_ready[l], lev + 1)
                    if l == 3:
                        act.wait_ge(thr_ready[3], 32 * (lev * G + 1))
                    if l == 3:
                        def first_group(c, closing=False):
                            hi(c)
                            act.wait_ge(parts_ready[l], lev * NBODY + c + 1)
                            next_parts(0, c, 0)
                            rest_of_body(0, c, closing)

                        steps(0, 0, (0, 2))
                        first_group(0)
                        with act.Fori(1, NBODY - 1) as c:
                            first_group(c)
                        first_group(NBODY - 1, closing=True)
                    else:
                        for first in (True, False):
                            with nullcontext(0) if first else act.Fori(1, NBODY) as c:
                                hi(c)
                                act.wait_ge(parts_ready[l], lev * NBODY + c + 1)
                                scale_upper(0, c, range(BODY))
                    with act.Fori(1, G) as g:
                        if l == 3:
                            act.wait_ge(thr_ready[3], 32 * (lev * G + g + 1))
                            steps(g, 0, (0, 2))
                            next_parts(g, 0, 0)
                            read_banks(g - 1)
                            rest_of_body(g, 0)
                            next_parts(g, 1, 0)
                            rest_of_body(g, 1)
                            elu(g - 1)
                            with act.Fori(2, NBODY - 1) as c:
                                next_parts(g, c, 0)
                                rest_of_body(g, c)
                            next_parts(g, NBODY - 1, 0)
                            rest_of_body(g, NBODY - 1, closing=True)
                        else:
                            scale_upper(g, 0, range(B16_RING - 1))
                            read_banks(g - 1)
                            scale_upper(g, 0, range(B16_RING - 1, BODY))
                            with act.Fori(1, NBODY) as c:
                                scale_upper(g, c, range(BODY))
                    read_banks(G - 1)
                    if l == 3:
                        elu(G - 1)

        @block.vector
        def _(dve):
            ve = nc.vector
            dve.wait_ge(w_loaded, 16 * 6)
            dve.wait_ge(w_trans, 1)
            ve.tensor_copy(w_t[:, :, :], psum[:, 5, 0:3 * P].rearrange("p (k d) -> p k d", k=3))
            dve.drain()
            in_out = [w_t[:, 0, :], w_raw[:, 1, :], w_raw[:, 2, :]]
            for k in range(3):
                ve.tensor_tensor(w_e[:, k, :], in_out[k], in_out[k], ALU.mult)
            dve.drain().then_inc(w_copied, 1)
            dve.wait_ge(w_proj, 1)
            ve.tensor_copy(w_a[:, :, :], psum[:, 6, 0:6].rearrange("p (k d) -> p k d", k=3))
            ve.tensor_reduce(one["n2"][:, :], psum[:, 7, 0:3 * P].rearrange("p (k d) -> p k d", k=3), AX_X, ALU.max)
            dve.drain().then_inc(norm2_ready, 1)
            dve.wait_ge(w_norm, 1)
            ve.tensor_scalar(one["n2"][:, :], one["n2"][:, :], LEAST, None, ALU.max)
            dve.drain()
            ve.tensor_scalar(one["p2"][:, :].bitcast(I32), one["n2"][:, :].bitcast(I32), EXP_BITS, None, ALU.bitwise_and)
            dve.drain()
            ve.tensor_scalar(one["unscale"][:, 0:2], one["p2"][:, 0:2], 1.0 / E_BOUND, None, ALU.mult)
            ve.tensor_scalar(one["unscale"][:, 2:3], one["p2"][:, 2:3], 1.0 / (E_BOUND * E_MORE), None, ALU.mult)
            dve.drain()
            ve.reciprocal(one["scale"][:, :], one["unscale"][:, :])
            ve.tensor_scalar(one["knorm"][:, :], one["unscale"][:, :], NORM_SCALE, None, ALU.mult)
            dve.drain()
            for k in range(3):
                ve.tensor_scalar(w_e[:, k, :], in_out[k], one["scale"][:, k:k + 1], None, ALU.mult)
            dve.drain().then_inc(w_ready, 1)

            def fold(parts, mu, var):
                m0, q0, m1, q1 = (parts[:, :, k] for k in (1, 2, 4, 5))
                d, q = parts[:, :, 0], parts[:, :, 3]
                dve.drain()
                ve.tensor_tensor(mu, m0, m1, ALU.add)
                ve.tensor_tensor(d, m0, m1, ALU.subtract)
                ve.tensor_tensor(q, q0, q1, ALU.add)
                dve.drain()
                ve.tensor_scalar(mu, mu, 0.5, None, ALU.mult)
                ve.tensor_tensor(d, d, d, ALU.mult)
                dve.drain()
                ve.scalar_tensor_tensor(out=q, in0=d, scalar=D / 4.0, in1=q, op0=ALU.mult, op1=ALU.add)
                dve.drain()
                ve.tensor_scalar(var, q, 1.0 / D, EPS, ALU.mult, ALU.add)

            def deviations(l):
                dve.drain().then_inc(var_ready, 1)
                dve.wait_ge(std_ready, l + 1)
                ve.reciprocal(vec["rstd"][:, :], vec["rstd"][:, :])
                dve.drain()

            def centre(l, unit, s, first):
                if not first:
                    dve.wait_ge(h_ready[l], unit - 1)
                for k in range(UB):
                    b = unit * UB + k
                    out = ve.tensor_scalar(hs[:, s, k * P:(k + 1) * P], x[:, bass.ds(b, 1), :].rearrange("p a w -> p (a w)"),
                                           vec["mu"][:, bass.ds(b, 1)], vec["rstd"][:, bass.ds(b, 1)],
                                           ALU.subtract, ALU.mult)
                out.then_inc(h_raw[l], 1)

            def make_mask(b, c, first=False):
                dve.wait_ge(adj_loaded[c], 16 * b + 16)
                if not first:
                    dve.wait_ge(packed, (b - 1) * NCOL + c + 1)
                ve.tensor_scalar(adj_bf[:, c, :], adj_sb[:, c, :], 0.0, None, ALU.is_gt).then_inc(adj_masked, 1)

            dve.wait_ge(x_loaded, 16)
            with dve.Fori(0, NB // 8) as i:
                for k in range(8):
                    ve.bn_stats(stats[:, bass.ds(i * 8 + k, 1), :].rearrange("p a w -> p (a w)"),
                                x[:, bass.ds(i * 8 + k, 1), :].rearrange("p a w -> p (a w)"))
            fold(stats, vec["mu"][:, :], vec["var"][:, :])
            deviations(0)
            dve.wait_ge(const_ready, 1)
            QUARTER = NB // UB // 4 // 2
            for quarter in range(4):
                for c in range(NCOL):
                    make_mask(quarter, c, first=(quarter == 0))
                for first in (True, False) if quarter == 0 else (False,):
                    begin, end = quarter * QUARTER + (quarter == 0), (quarter + 1) * QUARTER
                    if not first and begin == end:
                        continue
                    with nullcontext(0) if first else dve.Fori(begin, end) as i:
                        for s in range(2):
                            centre(0, 2 * i + s, s, first)
                        for s in range(2):
                            unit = 2 * i + s
                            dve.wait_ge(hi_ready, unit + 1)
                            hb = hr[:, s, :].rearrange("p (b d) -> p b d", b=UB)
                            at = bass.ds(unit * UB, UB)
                            ve.scalar_tensor_tensor(out=xu[:, at, 1, 0:D], in0=hb, scalar=H_SCALE, in1=xu[:, at, 0, 0:D],
                                                    op0=ALU.mult, op1=ALU.subtract)
                            ve.tensor_tensor(x[:, at, :], x[:, at, :], hb, ALU.add).then_inc(h_used, 1)

            def unpack(b, u, slot):
                dve.wait_ge(evacuated, b + 1 + 2)
                dve.wait_ge(sums_done, b + 1)
                for k in range(8):
                    pick(planes8[:, slot, k].bitcast(U16), packed8[:, u // 2, :, u % 2 * P:(u % 2 + 1) * P].bitcast(U16),
                         k).then_inc(planes, 1)

            def add_sums(b, slot, b_mod):
                dve.wait_ge(sums_done, b + 1 + 2)
                at = bass.ds(b, 1)
                xb = x[:, at, :].rearrange("p a w -> p (a w)")
                ve.scalar_tensor_tensor(out=xb, in0=psum[:, 4 + slot, 0:D], scalar=1.0 / (H_SCALE * MASK_F8),
                                        in1=xb, op0=ALU.mult, op1=ALU.add)
                ve.tensor_scalar(vec["empty"][:, at], psum[:, 4 + slot, NORM:NORM + 1], 0.0, None,
                                 ALU.is_equal).then_inc(sums_read, 1)
                dve.drain()
                ve.bn_stats(stats8[:, b_mod, :], xb)
                if b_mod == 3:
                    at = bass.ds(b - 3, 4)
                    fold(stats8[:, 0:4, :], vec["mu"][:, at], vec["var"][:, at])
                    dve.drain()

            for b in range(2):
                unpack(b, b, b)
            with dve.Fori(0, (NB - 4) // 4) as i:
                for u in range(4):
                    for c in range(NCOL):
                        make_mask(4 * i + u + 4, c)
                    add_sums(4 * i + u, u % 2, u)
                    unpack(4 * i + u + 2, (u + 2) % 4, u % 2)
            for u in range(4):
                add_sums(NB - 4 + u, u % 2, u)
                if u < 2:
                    unpack(NB - 2 + u, u + 2, u % 2)
            dve.drain()

            def first_pass(lev):
                v3 = [(vec["v"], vz[:, :, 0:3]), (vec["vl"], vz[:, :, 3:6])]
                for value, parts in v3:
                    ve.tensor_copy(parts[:, :, 0], value[:, :])
                    dve.drain()
                    ve.tensor_tensor(vec["rest"][:, :], value[:, :], parts[:, :, 0], ALU.subtract)
                    dve.drain()
                    ve.tensor_copy(parts[:, :, 1], vec["rest"][:, :])
                    dve.drain()
                    ve.tensor_tensor(vec["rest"][:, :], vec["rest"][:, :], parts[:, :, 1], ALU.subtract)
                    dve.drain()
                    ve.tensor_copy(parts[:, :, 2], vec["rest"][:, :])
                    dve.drain()
                ve.tensor_copy(vz[:, :, 6:9], vz[:, :, 3:6])
                ve.tensor_copy(vz[:, :, 9], vec["valid"][:, :])
                dve.drain().then_inc(z_parts, 1)

                def cut_upper(g, half, o, new_group):
                    c = half * HO + o
                    if new_group:
                        dve.wait_ge(z_thr_ready, 16 * (lev * G + g + 1))
                    dve.wait_ge(z_masks_ready[half], 16 * (lev * G + g + 1))
                    body, first = (lev * G + g) * NBODY + c, lev * TILES + g * NB + c * BODY

                    def unpack_pair(u0):
                        dve.wait_ge(z_tile, first + u0 + 2)
                        for u in (u0, u0 + 1):
                            pick(words4(C8[:, u, :]), mask_words(half, o), u).then_inc(z_unpacked, 1)

                    def step_pair(u0):
                        for u in (u0, u0 + 1):
                            if Z_ACT <= u < BODY:
                                dve.wait_ge(z_upper8, first + u + 1)
                                ve.tensor_scalar(z_step[:, u, :], splits_of(g), vec["t"][:, bass.ds(c * BODY + u, 1)],
                                                 float(MASK), ALU.is_le, ALU.mult).then_inc(z_stepped, 1)

                    unpack_pair(0)
                    for u0 in range(0, BODY, 2):
                        n0 = first + u0
                        step_pair(u0 + 2)
                        if u0 + 2 < BODY:
                            unpack_pair(u0 + 2)
                        dve.wait_ge(z_unpacked, n0 + 2 + NB)
                        if u0 < Z_ACT:
                            dve.wait_ge(z_act_stepped, (body + NBODY) * Z_ACT + min(u0 + 2, Z_ACT) + 1)
                        if u0 + 1 >= Z_ACT:
                            dve.wait_ge(z_stepped, (body + NBODY) * Z_DVE + u0 + 2 - Z_ACT + 1)
                        ve.tensor_tensor(two(B8, u0), two(z_step, u0), two(C8, u0), ALU.bitwise_and).then_inc(z_upper8, 2)

                with dve.Fori(0, G) as g:
                    cut_upper(g, 0, 0, True)
                    with dve.Fori(1, HO) as o:
                        cut_upper(g, 0, o, False)
                    with dve.Fori(0, HO) as o:
                        cut_upper(g, 1, o, False)

                dve.wait_ge(z_read, lev * G + G + 1)
                ve.tensor_reduce(zr[:, :, :], zs[:, :, 0:9].rearrange("p b (k w) -> p b k w", w=3), AX_X, ALU.add)
                dve.drain()
                ve.tensor_tensor(vec["rest"][:, :], zr[:, :, 2], zr[:, :, 1], ALU.subtract)
                dve.drain()
                ve.tensor_tensor(vec["rest"][:, :], vec["rest"][:, :], vec["clow"][:, :], ALU.mult)
                dve.drain()
                ve.tensor_tensor(vec["rest"][:, :], vec["rest"][:, :], zr[:, :, 0], ALU.add)
                dve.drain()
                ve.tensor_scalar(vec["rest"][:, :], vec["rest"][:, :], 1.0 / MASK_F8, None, ALU.mult)
                dve.drain()
                ve.tensor_scalar(vec["z"][:, :], vec["rest"][:, :], ROW_SUM_LEAST, None, ALU.max)
                ve.tensor_scalar(vec["new"][:, :], vec["rest"][:, :], ROW_SEEN[3], None, ALU.is_ge)
                ve.tensor_scalar(vec["tmp"][:, :], zs[:, :, 9], 0.0, None, ALU.is_equal)
                dve.drain()
                ve.reciprocal(vec["f"][:, :], vec["z"][:, :])
                ve.tensor_tensor(vec["new"][:, :], vec["new"][:, :], vec["tmp"][:, :], ALU.max)
                dve.drain().then_inc(row_sum, 1)
                ve.tensor_tensor(vec["new"][:, :], vec["new"][:, :], vec["done"][:, :], ALU.is_gt)
                ve.tensor_tensor(vec["f"][:, :], vec["f"][:, :], zs[:, :, 9], ALU.mult)
                dve.drain()
                ve.tensor_tensor(vec["done"][:, :], vec["done"][:, :], vec["new"][:, :], ALU.max)
                ve.tensor_scalar(vec["f"][:, :], vec["f"][:, :], one["unscale"][:, 2:3], 1.0 / MASK_F8 ** 2, ALU.mult, ALU.mult)
                dve.drain()
                ve.tensor_tensor(vec["f"][:, :], vec["f"][:, :], vec["new"][:, :], ALU.mult)
                dve.wait_ge(row_ln, lev + 1)
                ve.tensor_scalar(vec["z"][:, :], vec["z"][:, :], float(np.log(THR)), None, ALU.add)
                dve.drain()
                ve.tensor_tensor(vec["rest"][:, :], vec["z"][:, :], vec["lnc"][:, :], ALU.subtract)
                ve.tensor_scalar(vec["tmp"][:, :], vec["z"][:, :], top[:, 0:1], None, ALU.add)
                dve.drain()
                ve.tensor_scalar(vec["rest"][:, :], vec["rest"][:, :], 1.0 / SLOPE[3], top[:, 0:1], ALU.mult, ALU.add)
                ve.scalar_tensor_tensor(out=vec["tmp"][:, :], in0=vec["s"][:, :], scalar=-1.0, in1=vec["tmp"][:, :],
                                        op0=ALU.mult, op1=ALU.max)
                dve.drain()
                ve.tensor_tensor(vec["tmp2"][:, :], vec["rest"][:, :], vec["tmp"][:, :], ALU.min)
                dve.drain().then_inc(cuts, 1)
                dve.wait_ge(cuts_trans, lev + 1)
                dve.wait_ge(cut_stored, 16 * lev + 16)
                ve.tensor_copy(rows[:, :, :], psum[0:NB, 0, 0:2 * P].rearrange("b (k p) -> b k p", k=2)).then_inc(cut_rows, 1)

            for l in LAYERS:
                slope, kw = SLOPE[l], l - 1
                deviations(l)
                if l == 1:
                    for s in range(2):
                        dve.wait_ge(mask_stored[s], 16 * (NB // 4) + 16)
                NU = NB // UB

                def copy_hT(unit, s, first):
                    dve.wait_ge(h_trans[l], unit + 1)
                    if not first:
                        dve.wait_ge(e_made[l], unit - 1)
                    ve.tensor_copy(hT[:, s, :], psum[:, s, :]).then_inc(hT_ready[l], 1)

                for u in range(2):
                    centre(l, u, u, True)
                for u in range(2):
                    centre(l, u + 2, u, False)
                    copy_hT(u, u, True)
                with dve.Fori(1, NU // 2 - 1) as i:
                    for u in range(2):
                        centre(l, 2 * i + u + 2, u, False)
                        copy_hT(2 * i + u, u, False)
                for u in range(2):
                    copy_hT(NU - 2 + u, u, False)

                dve.wait_ge(e_ready[l], NU)
                st = e[:, :, D:EP]
                ve.tensor_copy(vec["s"][:, :], st[:, :, 0])
                ve.tensor_copy(vec["t"][:, :], st[:, :, 1])
                ve.tensor_scalar(vec["tmp"][:, :], st[:, :, 0], -1.0, None, ALU.mult)
                ve.tensor_scalar(vec["tmp2"][:, :], st[:, :, 1], -1.0, None, ALU.mult)
                dve.drain().then_inc(neg_s, 1)
                ve.tensor_reduce(tm[:, 0:1], vec["t"][:, :], AX_X, ALU.max)
                ve.tensor_reduce(tm[:, 1:2], vec["tmp2"][:, :], AX_X, ALU.max)
                dve.drain().then_inc(t_range, 1)
                ve.memset(vec["done"][:, :], 0.0)
                ve.memset(e[:, :, NORM:NORM + 1], NORM_SCALE)
                if l == 3:
                    ve.tensor_scalar(vec["t_far"][:, :], vec["t"][:, :], FAR, None, ALU.mult)
                dve.wait_ge(neg_s_trans, l)
                ve.tensor_copy(rows[:, 0, :], psum[0:NB, 5, 0:P]).then_inc(neg_s_row, 1)
                if l == 3:
                    ve.tensor_reduce(vec["valid"][:, :], e[:, :, 0:D], AX_X, ALU.add)
                    dve.drain()
                    ve.tensor_scalar(vec["valid"][:, :], vec["valid"][:, :], 0.0, None, ALU.not_equal)
                dve.wait_ge(t_range_all, l)
                ve.tensor_copy(top[:, :], tmr[:, 0:1])
                ve.tensor_tensor(levels_f[:, :], tmr[:, 0:1], tmr[:, 1:2], ALU.add)
                dve.drain()
                ve.tensor_scalar(levels_f[:, :], levels_f[:, :], 1.0 / WINDOW[l], 0.5, ALU.mult, ALU.add)
                dve.drain()
                ve.tensor_scalar(levels_f[:, :], levels_f[:, :], float(MAX_LEVELS), 1.0, ALU.min, ALU.max)
                dve.drain()
                ve.tensor_copy(levels[:, kw:kw + 1], levels_f[:, :])
                dve.drain().then_inc(levels_ready, 1)

                n_lev = n_levels(dve, l)
                with dve.Fori(0, n_lev) as lev:
                    ve.tensor_scalar(vec["tmp2"][:, :], vec["t"][:, :], top[:, 0:1], None, ALU.subtract)
                    ve.tensor_scalar(vec["lnc"][:, :], vec["s"][:, :], top[:, 0:1], 0.0, ALU.add, ALU.max)
                    dve.drain()
                    ve.tensor_scalar(vec["keep"][:, :], vec["tmp2"][:, :], 0.0, None, ALU.is_le)
                    dve.drain()
                    ve.tensor_scalar(vec["tmp2"][:, :], vec["tmp2"][:, :], 0.0, None, ALU.min)
                    ve.tensor_scalar(vec["lnc"][:, :], vec["lnc"][:, :], slope - 1.0, None, ALU.mult)
                    if l == 3:
                        ve.tensor_tensor(vec["keep"][:, :], vec["keep"][:, :], vec["valid"][:, :], ALU.mult)
                    dve.drain().then_inc(gaps_ready[l], 1)
                    dve.wait_ge(exps_ready[l], lev + 1)
                    ve.tensor_tensor(vec["v"][:, :], vec["v"][:, :], vec["keep"][:, :], ALU.mult)
                    ve.tensor_tensor(vec["vl"][:, :], vec["vl"][:, :], vec["keep"][:, :], ALU.mult)
                    if l != 3:
                        ve.tensor_scalar(vec["clow"][:, :], vec["clow"][:, :], 1.0 / MASK_F8, None, ALU.mult)
                    dve.drain()
                    ve.tensor_scalar(vec["pow2"][:, :].bitcast(I32), vec["v"][:, :].bitcast(I32), EXP_BITS, None,
                                     ALU.bitwise_and)
                    ve.tensor_scalar(vec["mant"][:, :].bitcast(I32), vec["v"][:, :].bitcast(I32), MANT_BITS, ONE_BITS,
                                     ALU.bitwise_and, ALU.bitwise_or)
                    dve.drain()
                    ve.tensor_scalar(vec["pow2"][:, :], vec["pow2"][:, :], 1.0 / MASK, None, ALU.mult)
                    dve.drain().then_inc(scales_ready[l], 1)

                    if l == 3:
                        first_pass(lev)

                    def parts(c):
                        at = bass.ds(c * GB, GB)
                        for k, scale in enumerate((vec["v"] if l == 3 else vec["mant"], vec["vl"])):
                            ve.tensor_tensor(tmp[:, k, :, :], e[:, at, 0:E], over(scale[:, at], E),
                                             ALU.mult).then_inc(prod_ready[l], 1)
                        for k, half in enumerate((xu, xl)):
                            dve.wait_ge(hi_done[l], lev * 2 * NBODY + 2 * c + k + 1)
                            out = ve.tensor_tensor(half[:, at, 1, 0:E], tmp[:, k, :, :], half[:, at, 0, 0:E], ALU.subtract)
                        out.then_inc(parts_ready[l], 1)

                    def cut_masks(g, half, o, opening=False, closing=False):
                        c = half * HO + o
                        if opening:
                            dve.wait_ge(thr_ready[l], 16 * (2 if l == 3 else 1) * (lev * G + g + 1))
                        dve.wait_ge(masks_ready[l][half], 16 * (lev * G + g + 1))
                        first = lev * TILES + g * NB + c * BODY

                        def steps(u0):
                            for u in (u0, u0 + 1):
                                t_of = vec["t"][:, bass.ds(c * BODY + u, 1)]
                                if l != 3:
                                    ve.tensor_scalar(step8[:, u % 4, :], splits_of(g), t_of, float(MASK),
                                                     ALU.is_le, ALU.mult).then_inc(stepped[l], 1)
                                elif u != u0:
                                    ve.tensor_scalar(step8[:, 4 + u % 4, :], thr[:, 1, :], t_of, float(MASK),
                                                     ALU.is_le, ALU.mult).then_inc(stepped[l], 2)

                        def lower(u0):
                            dve.wait_ge(upper8[l], first + u0 + 2 + 4)
                            ve.tensor_tensor(two(C8, u0), two(B8, u0), two(C8, u0), ALU.bitwise_xor).then_inc(lower8[l], 2)

                        if opening:
                            steps(0)
                        for u0 in range(0, BODY, 2):
                            n0 = first + u0
                            dve.wait_ge(tile_done[l], n0 + 2)
                            for u in (u0, u0 + 1):
                                pick(words4(C8[:, u, :]), mask_words(half, o), u).then_inc(unpacked[l], 1)
                            if u0 > 0:
                                lower(u0 - 2)
                            dve.wait_ge(stepped[l], n0 + 2 + NB + 1)
                            dve.wait_ge(unpacked[l], n0 + 2 + NB)
                            pair = (lev * G + g) * (NB // 2) + c * (BODY // 2) + u0 // 2
                            if l == 3:
                                dve.wait_ge(act_stepped, pair * N_ACT + 1 + 1)
                                ve.tensor_tensor(two(C8, u0), two(step8, 4 + u0 % 4), two(C8, u0), ALU.bitwise_and) \
                                    .then_inc(kept8, 2)
                                if u0 + 2 < BODY or not closing:
                                    steps(u0 + 2)
                                dve.wait_ge(act_stepped, pair * N_ACT + N_ACT + 1)
                                dve.wait_ge(kept8, n0 + 2)
                            else:
                                dve.wait_ge(upper16[l], n0 + 2)
                            ve.tensor_tensor(two(B8, u0), two(step8, u0 % 4), two(C8, u0), ALU.bitwise_and) \
                                .then_inc(upper8[l], 2)
                            if l != 3 and (u0 + 2 < BODY or not closing):
                                steps(u0 + 2)
                        lower(BODY - 2)

                    def finish(g):
                        at = bass.ds(g * GB, GB)
                        dve.wait_ge(bank_read[l], lev * NB + (g + 1) * GB + GB)
                        if l != 3:
                            dve.wait_ge(mean_added, l)
                        else:
                            dve.wait_ge(elu_added, lev * G + g + 1)
                        W = WIDTH[l]
                        ve.tensor_tensor(comb[:, :, 0:W], stage[:, :, W:2 * W], over(vec["clow"][:, at], W), ALU.mult)
                        dve.drain()
                        ve.tensor_tensor(comb[:, :, 0:W], comb[:, :, 0:W], stage[:, :, 0:W], ALU.add)
                        dve.drain().then_inc(stage_used[l], 1)
                        if l != 3:
                            new, f, done = vec["new"][:, at], vec["f"][:, at], vec["done"][:, at]
                            z = comb[:, :, NORM]
                            ve.tensor_scalar(new, z, ROW_SEEN[l] * NORM_SCALE, None, ALU.is_ge)
                            ve.tensor_scalar(f, z, LEAST, None, ALU.max)
                            dve.drain()
                            ve.tensor_tensor(new, new, done, ALU.is_gt)
                            ve.reciprocal(f, f)
                            dve.drain()
                            ve.tensor_tensor(done, done, new, ALU.max)
                            ve.scalar_tensor_tensor(out=f, in0=f, scalar=one["knorm"][:, kw:kw + 1], in1=new,
                                                    op0=ALU.mult, op1=ALU.mult)
                            dve.drain()
                        ve.tensor_tensor(y[:, :, :], comb[:, :, 0:D], over(vec["f"][:, at], D), ALU.mult)
                        dve.drain()

                    def add(g):
                        at = bass.ds(g * GB, GB)
                        if l == 1:
                            ve.tensor_scalar(y[:, :, :], y[:, :, :], 0.0, None, ALU.max)
                            dve.drain()
                        if l == 3:
                            ve.scalar_tensor_tensor(out=y[:, :, :], in0=e[:, at, 0:D], scalar=one["unscale"][:, kw:kw + 1],
                                                    in1=y[:, :, :], op0=ALU.mult, op1=ALU.add)
                            dve.drain()
                            ve.tensor_scalar(comb[:, :, 0:D], y[:, :, :], 0.0, None, ALU.min)
                            dve.drain().then_inc(elu_neg, 1)
                            ve.tensor_scalar(y[:, :, :], y[:, :, :], 0.0, -1.0, ALU.max, ALU.add).then_inc(elu_pos, 1)
                        else:
                            ve.tensor_tensor(x[:, at, :], x[:, at, :], y[:, :, :], ALU.add)
                        if l != 3:
                            dve.drain()
                            for k in range(GB):
                                ve.bn_stats(stats8[:, k, :], x[:, bass.ds(g * GB + k, 1), :].rearrange("p a w -> p (a w)"))
                            fold(stats8[:, :, :], vec["mu"][:, at], vec["var"][:, at])

                    parts(0)
                    cut_masks(0, 0, 0, opening=True)
                    with dve.Fori(1, HO) as o:
                        parts(o)
                        cut_masks(0, 0, o)
                    with dve.Fori(0, HO - 1) as o:
                        parts(o + HO)
                        cut_masks(0, 1, o)
                    parts(NBODY - 1)
                    cut_masks(0, 1, HO - 1, closing=True)
                    with dve.Fori(1, G) as g:
                        cut_masks(g, 0, 0, opening=True)
                        finish(g - 1)
                        cut_masks(g, 0, 1)
                        add(g - 1)
                        if HO > 2:
                            with dve.Fori(2, HO) as o:
                                cut_masks(g, 0, o)
                        with dve.Fori(0, HO - 1) as o:
                            cut_masks(g, 1, o)
                        cut_masks(g, 1, HO - 1, closing=True)
                    finish(G - 1)
                    add(G - 1)
                    dve.drain()
                    if l == 3:
                        dve.wait_ge(elu_added, lev * G + G + 1)
                    ve.tensor_scalar(top[:, :], top[:, :], -WINDOW[l], None, ALU.add)
                    dve.drain()
            dve.drain().then_inc(x_final, 1)


_INS = ["x", "adj", "L1_gnn_W", "L1_gnn_a", "L2_gnn_W", "L2_gnn_a", "L3_gnn_W", "L3_gnn_a"]


def kernel(**inputs):
    import numpy as _np
    import concourse.bacc as _bacc
    from concourse import mybir as _mybir
    from concourse.bass_utils import run_bass_kernel_spmd as _run

    nc = _bacc.Bacc("TRN2", target_bir_lowering=False, num_devices=1)
    arrays, args = {}, []
    for name in _INS:
        a = _np.ascontiguousarray(inputs[name])
        arrays[f"in_{name}_dram"] = a
        args.append(nc.dram_tensor(f"in_{name}_dram", a.shape, _mybir.dt.from_np(a.dtype), kind="ExternalInput").ap())
    out = nc.dram_tensor("out_0_dram", inputs["x"].shape, _mybir.dt.from_np(_np.dtype("float32")), kind="ExternalOutput").ap()
    build_layers(nc, *args, out)
    r = _run(nc, [arrays], core_ids=[0])
    return r.results[0]["out_0_dram"]
```
